# Optimizing a Trainium2 kernel written in Bass

```python
import numpy as np
import jax
import jax.numpy as jnp

def _softmax(x, axis=-1):
    return jax.nn.softmax(x, axis=axis)

def _gelu(x):
    return jax.nn.gelu(x, approximate=True)

def _silu(x):
    return jax.nn.silu(x)

def _sigmoid(x):
    return jax.nn.sigmoid(x)

def _layernorm(x, axis=-1, eps=1e-05):
    m = jnp.mean(x, axis=axis, keepdims=True)
    v = jnp.var(x, axis=axis, keepdims=True)
    return (x - m) / jnp.sqrt(v + eps)

def _scatter_add(tgt, idx, src, axis=0):
    return tgt.at[idx].add(src)

def _segment_sum(src, seg, n):
    return jax.ops.segment_sum(src, seg, n)
kernel_name = 'mk_macaron_d1_jaxref_r8_12f43a'

def setup_inputs(seed: int=0):
    np.random.seed(seed)
    _w = jnp.asarray

    def _L0_attn_setup():
        import jax, jax.numpy as jnp
        import numpy as np

        def _rope_cos_sin(m, d, dtype=jnp.float32):
            i = jnp.arange(d // 2, dtype=dtype)
            theta = jnp.power(jnp.asarray(10000.0, dtype), -2.0 * (i - 1.0) / d)
            pos = jnp.arange(m, dtype=dtype)
            ang = pos[:, None] * theta[None, :]
            return (jnp.cos(ang), jnp.sin(ang))

        def _rotate(t, cos, sin):
            te = t[..., 0::2]
            to = t[..., 1::2]
            re = te * cos + to * sin
            ro = -te * sin + to * cos
            return jnp.stack((re, ro), axis=-1).reshape(t.shape)
        key = jax.random.key(seed)
        k1, k2, k3, k4 = jax.random.split(key, 4)
        b, m, d = (4, 256, 128)
        scale = 1.0 / np.sqrt(d)
        return {'x': jax.random.normal(k1, (b, m, d), dtype=jnp.float32), 'w_q': jax.random.normal(k2, (d, d), dtype=jnp.float32) * scale, 'w_k': jax.random.normal(k3, (d, d), dtype=jnp.float32) * scale, 'w_v': jax.random.normal(k4, (d, d), dtype=jnp.float32) * scale}
    _L0_attn_in = _L0_attn_setup()

    def _L0_ffn_setup():
        import jax, jax.numpy as jnp
        import numpy as np
        from jax import lax
        DIM = 128
        INTER = 64
        N_EXPERTS = 16
        TOPK = 4
        ROUTE_SCALE = 2.5
        VOCAB = 4000

        def _silu_and_mul(gu):
            gate, up = jnp.split(gu, 2, axis=-1)
            return jax.nn.silu(gate) * up
        key = jax.random.key(seed)
        ks = jax.random.split(key, 8)
        x = jax.random.normal(ks[0], (2, 64, DIM), dtype=jnp.float32)
        input_ids = jax.random.randint(ks[1], (2, 64), 0, VOCAB)
        s = 0.02
        gate_w = jax.random.normal(ks[2], (N_EXPERTS, DIM), dtype=jnp.float32) * s
        gate_b = jax.random.normal(ks[3], (N_EXPERTS,), dtype=jnp.float32) * s
        w13 = jax.random.normal(ks[4], (N_EXPERTS, 2 * INTER, DIM), dtype=jnp.float32) * s
        w2 = jax.random.normal(ks[5], (N_EXPERTS, DIM, INTER), dtype=jnp.float32) * s
        w13_s = jax.random.normal(ks[6], (2 * INTER, DIM), dtype=jnp.float32) * s
        w2_s = jax.random.normal(ks[7], (DIM, INTER), dtype=jnp.float32) * s
        return {'x': x, 'input_ids': input_ids, 'gate_w': gate_w, 'gate_b': gate_b, 'w13': w13, 'w2': w2, 'w13_s': w13_s, 'w2_s': w2_s}
    _L0_ffn_in = _L0_ffn_setup()
    _d = {'L0_attn_x': _L0_attn_in['x'], 'L0_attn_w_q': _L0_attn_in['w_q'], 'L0_attn_w_k': _L0_attn_in['w_k'], 'L0_attn_w_v': _L0_attn_in['w_v'], 'L0_ffn_input_ids': _L0_ffn_in['input_ids'], 'L0_ffn_gate_w': _L0_ffn_in['gate_w'], 'L0_ffn_gate_b': _L0_ffn_in['gate_b'], 'L0_ffn_w13': _L0_ffn_in['w13'], 'L0_ffn_w2': _L0_ffn_in['w2'], 'L0_ffn_w13_s': _L0_ffn_in['w13_s'], 'L0_ffn_w2_s': _L0_ffn_in['w2_s']}
    _x0 = _d['L0_attn_x']
    _d['L0_attn_x'] = jax.random.normal(jax.random.fold_in(jax.random.key(seed), 1), (8, 1024, 128), dtype=_x0.dtype)
    del _x0
    return _d

def reference(L0_attn_x, L0_attn_w_q, L0_attn_w_k, L0_attn_w_v, L0_ffn_input_ids, L0_ffn_gate_w, L0_ffn_gate_b, L0_ffn_w13, L0_ffn_w2, L0_ffn_w13_s, L0_ffn_w2_s):

    def _L0_attn_ref(x, w_q, w_k, w_v):
        import jax, jax.numpy as jnp
        import numpy as np

        def _rope_cos_sin(m, d, dtype=jnp.float32):
            i = jnp.arange(d // 2, dtype=dtype)
            theta = jnp.power(jnp.asarray(10000.0, dtype), -2.0 * (i - 1.0) / d)
            pos = jnp.arange(m, dtype=dtype)
            ang = pos[:, None] * theta[None, :]
            return (jnp.cos(ang), jnp.sin(ang))

        def _rotate(t, cos, sin):
            te = t[..., 0::2]
            to = t[..., 1::2]
            re = te * cos + to * sin
            ro = -te * sin + to * cos
            return jnp.stack((re, ro), axis=-1).reshape(t.shape)
        b, m, d = x.shape
        q = jnp.einsum('bmd,ed->bme', x, w_q)
        k = jnp.einsum('bmd,ed->bme', x, w_k)
        v = jnp.einsum('bmd,ed->bme', x, w_v)
        cos, sin = _rope_cos_sin(m, d, x.dtype)
        q_rot = _rotate(q, cos, sin)
        k_rot = _rotate(k, cos, sin)
        scores = jnp.einsum('bqd,bkd->bqk', q_rot, k_rot) / jnp.sqrt(jnp.asarray(d, x.dtype))
        causal = jnp.tril(jnp.ones((m, m), dtype=bool))
        scores = jnp.where(causal[None], scores, jnp.asarray(-jnp.inf, scores.dtype))
        attn = jax.nn.softmax(scores, axis=-1)
        return jnp.einsum('bqk,bkd->bqd', attn, v)

    def _L0_ffn_ref(x, input_ids, gate_w, gate_b, w13, w2, w13_s, w2_s):
        import jax, jax.numpy as jnp
        import numpy as np
        from jax import lax
        DIM = 128
        INTER = 64
        N_EXPERTS = 16
        TOPK = 4
        ROUTE_SCALE = 2.5
        VOCAB = 4000

        def _silu_and_mul(gu):
            gate, up = jnp.split(gu, 2, axis=-1)
            return jax.nn.silu(gate) * up
        B, S, D = x.shape
        xt = x.reshape(-1, D)
        T = xt.shape[0]
        scores = jax.nn.sigmoid(xt.astype(jnp.float32) @ gate_w.T)
        biased = scores + gate_b
        _, idx = lax.top_k(biased, TOPK)
        w = jnp.take_along_axis(scores, idx, axis=-1)
        w = w / jnp.sum(w, axis=-1, keepdims=True)
        w = w * ROUTE_SCALE
        comb = jnp.zeros((T, N_EXPERTS), jnp.float32)
        comb = comb.at[jnp.arange(T)[:, None], idx].add(w)
        comb = comb.astype(x.dtype)

        def expert_body(y, args):
            w13_e, w2_e, c_e = args
            h = _silu_and_mul(xt @ w13_e.T)
            return (y + c_e[:, None] * (h @ w2_e.T), None)
        y, _ = lax.scan(expert_body, jnp.zeros_like(xt), (w13, w2, comb.T))
        y = y + _silu_and_mul(xt @ w13_s.T) @ w2_s.T
        return y.astype(x.dtype).reshape(B, S, D)
    x = L0_attn_x
    x = x + 0.5 * _L0_ffn_ref(_layernorm(x, axis=-1), L0_ffn_input_ids, L0_ffn_gate_w, L0_ffn_gate_b, L0_ffn_w13, L0_ffn_w2, L0_ffn_w13_s, L0_ffn_w2_s)
    x = x + _L0_attn_ref(_layernorm(x, axis=-1), L0_attn_w_q, L0_attn_w_k, L0_attn_w_v)
    x = x + 0.5 * _L0_ffn_ref(_layernorm(x, axis=-1), L0_ffn_input_ids, L0_ffn_gate_w, L0_ffn_gate_b, L0_ffn_w13, L0_ffn_w2, L0_ffn_w13_s, L0_ffn_w2_s)
    return x

_drawn_inputs = setup_inputs


def setup_inputs(seed=0):
    import zlib

    import numpy as np

    out = dict(_drawn_inputs(seed))
    spreads = {}
    factors = {'L0_ffn_gate_w': 8.0,
     'L0_ffn_gate_b': 8.0,
     'L0_ffn_w13': 8.0,
     'L0_ffn_w2': 8.0,
     'L0_ffn_w13_s': 8.0,
     'L0_ffn_w2_s': 8.0}
    for name, (base, spread) in spreads.items():
        noise = np.random.default_rng([zlib.crc32(name.encode()), seed]).standard_normal(out[name].shape)
        drawn = base * np.exp(spread * noise) if base else spread * noise
        out[name] = jnp.asarray(drawn.astype(out[name].dtype))
    for name, factor in factors.items():
        out[name] = (out[name] * factor).astype(out[name].dtype)
    return out
```

```python
from contextlib import ExitStack

import numpy as np

import concourse.bass as bass
from concourse import mybir

P = 128
B, M, D = 8, 1024, 128
INTER, NEXP, TOPK = 64, 16, 4
ROUTE_SCALE = 2.5
EPS = 1e-5
TILE = 512
NB = TILE // P
TILES = B * M // TILE
PAIRS = NEXP * INTER // P
UNITS = PAIRS + 1
QB = M // P
SCORE_SCALE = float(1.0 / np.sqrt(np.float32(D)))
MASKED = -3.0e38
SENTINEL, TAKEN = -3.0e38, 3.0e38
TINY = 1.0e-30
ROUTE = 16
PT_CHUNKS = 12

F32 = mybir.dt.float32
F32R = mybir.dt.float32r
ALU = mybir.AluOpType
ACT = mybir.ActivationFunctionType
AX_X = mybir.AxisListType.X

G_BANK, C_BANK, U_BANK, Y_BANK, T_BANK = (0, 1), (2, 3), (4, 5), 6, 7
PT_BANK, O_BANK, M_BANK = (4, 5), 6, 7

PREP_ITEMS = [("xnT", 0), ("xnT", 1), ("qkv", 0), ("qkv", 1), ("qkv", 2), ("qkT", 0), ("qkv", 3),
              ("qkv", 4), ("qkT", 1), ("qkv", 5), ("qkv", 6), ("qkT", 2), ("qkv", 7), ("qkT", 3)]


def prep_item(step, slot):
    return PREP_ITEMS[2 * (step - 1) + slot] if step >= 1 else None


def macaron(nc, x, w13T, w2T, wqkvT, gwT, gate_b, ident_d, sel_d, mask_d, cos_d, sin_d, out):
    x_v = x.rearrange("b (n p) d -> p (b n) d", p=P)
    out_v = out.rearrange("b (n p) d -> p (b n) d", p=P)

    with ExitStack() as ctx:
        def sb(name, shape, dt=F32):
            return ctx.enter_context(nc.sbuf_tensor(name, shape, dt))

        def sem(name):
            return ctx.enter_context(nc.semaphore(name))

        bank = ctx.enter_context(nc.psum_tensor("bank", [P, 8, 512], F32))

        X = sb("X", [P, B * QB, D])
        ident = sb("ident", [P, P])
        w13_f = sb("w13_f", [P, UNITS * 2 - 1, P])
        w13_h = sb("w13_h", [P, UNITS * 2 - 1, P], F32R)
        w13_l = sb("w13_l", [P, UNITS * 2 - 1, P], F32R)
        w2 = sb("w2", [P, UNITS, D])
        wqkv_f = sb("wqkv_f", [P, 3 * D])
        wqkv_h = sb("wqkv_h", [P, 3 * D], F32R)
        wqkv_l = sb("wqkv_l", [P, 3 * D], F32R)
        gw_f = sb("gw_f", [P, NEXP])
        gw_h = sb("gw_h", [P, NEXP], F32R)
        gw_l = sb("gw_l", [P, NEXP], F32R)
        gb = sb("gb", [P, NEXP])
        sel_f = sb("sel_f", [P, PAIRS, P])
        sel = sb("sel", [P, PAIRS, P], F32R)
        mask_f = sb("mask_f", [P, P])
        mask = sb("mask", [P, P], F32R)
        ident_r = sb("ident_r", [P, P], F32R)
        cos = sb("cos", [P, QB, D])
        sin = sb("sin", [P, QB, D])
        neg_half = sb("neg_half", [P, QB])

        stats = sb("stats", [P, QB, 6])
        mv = sb("mv", [P, QB, 2])
        var_eps = sb("var_eps", [P, QB])
        rstd = sb("rstd", [P, QB])
        xn = sb("xn", [P, QB, D])
        xh = [sb(f"xh{q}", [P, TILE], F32R) for q in range(2)]
        xl = [sb(f"xl{q}", [P, TILE], F32R) for q in range(2)]

        near0 = sb("near0", [P, NB, NEXP])
        logit = sb("logit", [P, NB, NEXP])
        gsilu = sb("gsilu", [P, NB, NEXP])
        rlogit = sb("rlogit", [P, NB, NEXP])
        score = sb("score", [P, NB, NEXP])
        biased = sb("biased", [P, NB, NEXP + TOPK])
        top8 = sb("top8", [P, NB, 8])
        take = sb("take", [P, NB, 8])
        marked = sb("marked", [P, NB, NEXP + TOPK])
        chosen = sb("chosen", [P, NB, NEXP])
        wsel = sb("wsel", [P, NB, NEXP])
        wsum = sb("wsum", [P, NB])
        rsum = sb("rsum", [P, NB])
        comb = sb("comb", [P, NB, NEXP])
        comb_hl = sb("comb_hl", [P, NB, P], F32R)
        combT = [sb(f"combT{q}", [P, TILE], F32R) for q in range(2)]

        silu = [sb(f"silu{q}", [P, TILE]) for q in range(2)]
        weighted = [sb(f"weighted{q}", [P, TILE]) for q in range(2)]
        h = [sb(f"h{q}", [P, TILE]) for q in range(3)]
        yT = sb("yT", [P, TILE])

        qkv = [sb(f"qkv{p}", [P, QB, 3 * D]) for p in range(2)]
        rope_c = [sb(f"rope_c{p}", [P, 2, D]) for p in range(2)]
        rope_s = [sb(f"rope_s{p}", [P, 2, D]) for p in range(2)]
        rot = [sb(f"rot{p}", [P, 2, D]) for p in range(2)]
        qkT_h = [sb(f"qkT_h{p}", [P, 2, M], F32R) for p in range(2)]
        qkT_l = [sb(f"qkT_l{p}", [P, 2, M], F32R) for p in range(2)]
        rowmax = [sb(f"rowmax{p}", [P, 1]) for p in range(2)]
        negmax = [sb(f"negmax{p}", [P, 1]) for p in range(2)]
        rowsum = [sb(f"rowsum{p}", [P, QB]) for p in range(2)]
        rrow = [sb(f"rrow{p}", [P, QB]) for p in range(2)]
        prob = [sb(f"prob{p}", [P, M]) for p in range(2)]
        probT = [sb(f"probT{p}", [P, QB, P]) for p in range(2)]

        weights_loaded = sem("weights_loaded")
        x_loaded = [sem(f"x_loaded{q}") for q in range(2)]
        consts_set = sem("consts_set")
        hi_set = sem("hi_set")
        weights_split = sem("weights_split")
        stats_done = sem("stats_done")
        mv_done = sem("mv_done")
        var_done = sem("var_done")
        rstd_done = sem("rstd_done")
        xn_done = sem("xn_done")
        xnT_ready = sem("xnT_ready")
        xh_done = sem("xh_done")
        xl_done = sem("xl_done")
        logits_ready = sem("logits_ready")
        gsilu_done = sem("gsilu_done")
        route_step = sem("route_step")
        combT_ready = sem("combT_ready")
        combT_done = sem("combT_done")
        gate_ready = sem("gate_ready")
        comb_ready = sem("comb_ready")
        up_ready = sem("up_ready")
        silu_done = sem("silu_done")
        weighted_done = sem("weighted_done")
        h_done = sem("h_done")
        down_done = sem("down_done")
        yT_done = sem("yT_done")
        y_ready = sem("y_ready")
        x_done = sem("x_done")
        stored = sem("stored")
        a_stats_done = sem("a_stats_done")
        a_mv_done = sem("a_mv_done")
        a_var_done = sem("a_var_done")
        a_rstd_done = sem("a_rstd_done")
        a_xn_done = sem("a_xn_done")
        a_xnT_ready = sem("a_xnT_ready")
        a_xh_done = sem("a_xh_done")
        a_xl_done = sem("a_xl_done")
        qkv_ready = sem("qkv_ready")
        qkv_done = sem("qkv_done")
        rope_c_done = sem("rope_c_done")
        rope_s_done = sem("rope_s_done")
        rot_done = sem("rot_done")
        qkT_ready = sem("qkT_ready")
        qkT_h_done = sem("qkT_h_done")
        qkT_l_done = sem("qkT_l_done")
        scores_ready = sem("scores_ready")
        rowmax_done = sem("rowmax_done")
        negmax_done = sem("negmax_done")
        exp_done = sem("exp_done")
        probT_ready = sem("probT_ready")
        probT_done = sem("probT_done")
        pv_ready = sem("pv_ready")
        rrow_done = sem("rrow_done")
        attn_done = sem("attn_done")

        WEIGHT_LOADS = 11
        SPLITS = 3

        def wait(eng, s, n):
            if not isinstance(n, int) or n > 0:
                eng.wait_ge(s, n)

        def tile_blocks(T):
            return bass.ds(NB * T, NB)

        block = ctx.enter_context(nc.Block())

        @block.sync
        def _(sp):
            sp.dma_start(X[:, 0:NB, :], x_v[:, 0:NB, :]).then_inc(x_loaded[0], 16)
            sp.dma_start(ident[:], ident_d).then_inc(weights_loaded, 16)
            sp.dma_start(gw_f[:], gwT).then_inc(weights_loaded, 16)
            sp.dma_start(gb[:], gate_b).then_inc(weights_loaded, 16)
            sp.dma_start(w13_f[:], w13T).then_inc(weights_loaded, 16)
            sp.dma_start(sel_f[:], sel_d).then_inc(weights_loaded, 16)
            sp.dma_start(w2[:], w2T).then_inc(weights_loaded, 16)
            sp.dma_start(X[:, NB:2 * NB, :], x_v[:, NB:2 * NB, :]).then_inc(x_loaded[1], 16)
            sp.dma_start(wqkv_f[:], wqkvT).then_inc(weights_loaded, 16)
            sp.dma_start(mask_f[:], mask_d).then_inc(weights_loaded, 16)
            sp.dma_start(cos[:], cos_d).then_inc(weights_loaded, 16)
            sp.dma_start(sin[:], sin_d).then_inc(weights_loaded, 16)
            sp.dma_start(neg_half[:], cos_d[:, 0, 0:QB]).then_inc(weights_loaded, 16)
            with sp.Fori(1, TILES // 2) as k:
                for q in range(2):
                    sp.wait_ge(x_loaded[q], 16 * k)
                    sp.dma_start(X[:, tile_blocks(2 * k + q), :],
                                 x_v[:, tile_blocks(2 * k + q), :]).then_inc(x_loaded[q], 16)
            with sp.Fori(0, TILES) as t:
                sp.wait_ge(x_done, TILES + 1 + t)
                sp.dma_start(out_v[:, tile_blocks(t), :], X[:, tile_blocks(t), :]).then_inc(stored, 16)
            sp.wait_ge(stored, 16 * TILES)

        @block.gpsimd
        def _(pool):
            nc.gpsimd.memset(take[:], SENTINEL).then_inc(consts_set, 1)
            nc.gpsimd.memset(biased[:], SENTINEL).then_inc(consts_set, 1)
            nc.gpsimd.memset(comb_hl[:].bitcast(mybir.dt.uint32), 0).then_inc(consts_set, 1)
            pool.wait_ge(weights_loaded, 16 * WEIGHT_LOADS)
            nc.gpsimd.memset(neg_half[:], -0.5).then_inc(consts_set, 1)
            pool.wait_ge(consts_set, 4)

            def ffn_rstd(T):
                pool.wait_ge(var_done, T + 1)
                nc.gpsimd.tensor_tensor(rstd[:, 0:NB], var_eps[:, 0:NB], neg_half[:, 0:NB],
                                        ALU.pow).then_inc(rstd_done, 1)

            def attn_rstd(b):
                pool.wait_ge(a_var_done, b + 1)
                nc.gpsimd.tensor_tensor(rstd[:], var_eps[:], neg_half[:], ALU.pow).then_inc(a_rstd_done, 1)

            def rope(b, p, n):
                s = n % 2
                pool.wait_ge(qkv_done, QB * b + n + 1)
                src = qkv[p][:, n, 0:2 * D].rearrange("p (w i e) -> p w i e", w=2, e=2)[:, :, :, ::-1]
                sn = sin[:, n, :].rearrange("p (w i e) -> p w i e", w=1, e=2).to_broadcast([P, 2, D // 2, 2])
                nc.gpsimd.tensor_tensor(rope_s[s][:].rearrange("p w (i e) -> p w i e", e=2), src, sn,
                                        ALU.mult).then_inc(rope_s_done, 1)
                pool.wait_ge(rope_s_done, QB * b + n + 1)
                pool.wait_ge(rope_c_done, QB * b + n + 1)
                if n >= 2:
                    pool.wait_ge(qkT_ready, QB // 2 * b + n // 2)
                else:
                    wait(pool, qkT_ready, QB // 2 * b)
                nc.gpsimd.tensor_tensor(rot[s][:], rope_c[s][:], rope_s[s][:], ALU.add).then_inc(rot_done, 1)

            def attn_prep(b, p):
                attn_rstd(b)
                for n in range(QB):
                    rope(b, p, n)

            ffn_rstd(0)
            with pool.Fori(1, TILES) as t:
                ffn_rstd(t)
            attn_prep(0, 0)
            with pool.Fori(0, B // 2 - 1) as k:
                attn_prep(2 * k + 1, 1)
                attn_prep(2 * k + 2, 0)
            attn_prep(B - 1, 1)
            with pool.Fori(TILES, 2 * TILES) as t:
                ffn_rstd(t)

        @block.scalar
        def _(act):
            def copy(dst, src):
                return nc.scalar.activation(dst, src, ACT.Copy)

            act.wait_ge(weights_loaded, 16 * WEIGHT_LOADS)
            copy(gw_h[:], gw_f[:]).then_inc(hi_set, 1)
            copy(w13_h[:], w13_f[:]).then_inc(hi_set, 1)
            copy(wqkv_h[:], wqkv_f[:]).then_inc(hi_set, 1)
            copy(sel[:], sel_f[:]).then_inc(hi_set, 1)
            copy(mask[:], mask_f[:]).then_inc(hi_set, 1)
            copy(ident_r[:], ident[:]).then_inc(hi_set, 1)

            def ffn_xh(T, q):
                act.wait_ge(xnT_ready, T + 1)
                copy(xh[q][:], bank[:, T_BANK, :]).then_inc(xh_done, 1)

            def ffn_gsilu(T):
                act.wait_ge(route_step, ROUTE * T + 3)
                nc.scalar.activation(gsilu[:], logit[:], ACT.Silu).then_inc(gsilu_done, 1)

            def ffn_combT(T, q):
                act.wait_ge(combT_ready, T + 1)
                copy(combT[q][:], bank[:, T_BANK, :]).then_inc(combT_done, 1)

            def ffn_silu(T, q, j):
                g = (q + j) % 2
                rows = P if j < PAIRS else INTER
                act.wait_ge(gate_ready, UNITS * T + j + 1)
                if j >= 2:
                    act.wait_ge(weighted_done, PAIRS * T + j - 1)
                elif j == 1:
                    wait(act, h_done, UNITS * T)
                else:
                    wait(act, weighted_done, PAIRS * T)
                nc.scalar.activation(silu[g][0:rows, :], bank[0:rows, G_BANK[g], :], ACT.Silu).then_inc(silu_done, 1)

            def ffn_yT(T):
                act.wait_ge(down_done, UNITS * (T + 1))
                wait(act, y_ready, T)
                copy(yT[:], bank[:, Y_BANK, :]).then_inc(yT_done, 1)

            def ffn_tile(T, q, first, last):
                for j in range(UNITS):
                    ffn_silu(T, q, j)
                    if j == 1 and not first:
                        ffn_yT(T - 1)
                    if j == 2 and not last:
                        ffn_xh(T + 1, 1 - q)
                    if j == 4 and not last:
                        ffn_gsilu(T + 1)
                    if j == UNITS - 1 and not last:
                        ffn_combT(T + 1, 1 - q)

            def ffn(base):
                ffn_xh(base, 0)
                ffn_gsilu(base)
                ffn_combT(base, 0)
                ffn_tile(base, 0, True, False)
                with act.Fori(0, TILES // 2 - 1) as k:
                    ffn_tile(base + 2 * k + 1, 1, False, False)
                    ffn_tile(base + 2 * k + 2, 0, False, False)
                ffn_tile(base + TILES - 1, 1, False, True)
                ffn_yT(base + TILES - 1)

            def attn_item(item, b, p):
                kind, n = item
                if kind == "xnT":
                    act.wait_ge(a_xnT_ready, 2 * b + n + 1)
                    copy(xh[n][:], bank[:, M_BANK, :]).then_inc(a_xh_done, 1)
                elif kind == "qkv":
                    act.wait_ge(qkv_ready, QB * b + n + 1)
                    copy(qkv[p][:, n, :], bank[:, M_BANK, 0:3 * D]).then_inc(qkv_done, 1)
                else:
                    act.wait_ge(qkT_ready, QB // 2 * b + n + 1)
                    copy(qkT_h[p][:, :, 2 * P * n:2 * P * (n + 1)],
                         bank[:, M_BANK, :].rearrange("p (w c) -> p w c", w=2)).then_inc(qkT_h_done, 1)

            def attn_exp(b, p, i):
                s, w = i % 2, (i + 1) * P
                act.wait_ge(negmax_done, QB * b + i + 1)
                if i >= 2:
                    act.wait_ge(probT_ready, PT_CHUNKS * b + chunk_index(i - 2, 1) + 1)
                else:
                    wait(act, probT_ready, PT_CHUNKS * (b - 1) + chunk_index(QB - 2 + i, 1) + 1)
                nc.scalar.activation(prob[s][:, 0:w],
                                     bank[:, 2 * s:2 * s + 2, :].rearrange("p a c -> p (a c)")[:, 0:w],
                                     ACT.Exp, bias=negmax[s][:], scale=SCORE_SCALE,
                                     accum_out=rowsum[p][:, i:i + 1]).then_inc(exp_done, 1)

            def attn_probT(b, i, c):
                s, m = i % 2, chunk_index(i, c)
                blocks = min(4, i + 1 - 4 * c)
                act.wait_ge(probT_ready, PT_CHUNKS * b + m + 1)
                if c == 0 and i >= 2:
                    act.wait_ge(pv_ready, QB * b + i - 1)
                elif c == 0:
                    wait(act, pv_ready, QB * (b - 1) + QB - 1 + i)
                copy(probT[s][:, 4 * c:4 * c + blocks, :].rearrange("p a c -> p (a c)"),
                     bank[:, PT_BANK[m % 2], 0:blocks * P]).then_inc(probT_done, 1)

            def attn_batch(b, p, last):
                for i in range(QB):
                    if not last and i >= 1:
                        attn_item(prep_item(i, 0), b + 1, 1 - p)
                    for c in range(1 + i // 4):
                        attn_probT(b, i, c)
                    if i + 1 < QB:
                        attn_exp(b, p, i + 1)
                    elif not last:
                        attn_exp(b + 1, 1 - p, 0)
                    if not last and i >= 1:
                        attn_item(prep_item(i, 1), b + 1, 1 - p)

            ffn(0)
            for item in PREP_ITEMS:
                attn_item(item, 0, 0)
            attn_exp(0, 0, 0)
            attn_batch(0, 0, False)
            with act.Fori(0, B // 2 - 1) as k:
                attn_batch(2 * k + 1, 1, False)
                attn_batch(2 * k + 2, 0, False)
            attn_batch(B - 1, 1, True)
            ffn(TILES)

        @block.vector
        def _(dve):
            dve.wait_ge(hi_set, 3)
            for f, hi, lo in ((gw_f, gw_h, gw_l), (w13_f, w13_h, w13_l), (wqkv_f, wqkv_h, wqkv_l)):
                nc.vector.tensor_tensor(lo[:], f[:], hi[:].bitcast(F32), ALU.subtract).then_inc(weights_split, 1)
            dve.wait_ge(consts_set, 4)

            def ln_stats(blocks, first_block, done):
                for n in range(blocks):
                    ins = nc.vector.bn_stats(stats[:, n, :], X[:, bass.ds(first_block + n, 1), :].rearrange("p a d -> p (a d)"))
                ins.then_inc(done, 1)

            def ln_mean_var(blocks, count, mv_sem, var_sem):
                for n in range(blocks):
                    ins = nc.vector.bn_aggr(mv[:, n, :], stats[:, n, :])
                ins.then_inc(mv_sem, 1)
                dve.wait_ge(mv_sem, count)
                nc.vector.tensor_scalar_add(var_eps[:, 0:blocks], mv[:, 0:blocks, 1], EPS).then_inc(var_sem, 1)

            def ln_apply(blocks, first_block, done):
                for n in range(blocks):
                    ins = nc.vector.tensor_scalar(xn[:, n, :], X[:, bass.ds(first_block + n, 1), :].rearrange("p a d -> p (a d)"),
                                                  mv[:, n, 0:1], rstd[:, n:n + 1], ALU.subtract, ALU.mult)
                ins.then_inc(done, 1)

            def ffn_xl(T, q):
                dve.wait_ge(xh_done, T + 1)
                nc.vector.tensor_tensor(xl[q][:], bank[:, T_BANK, :], xh[q][:].bitcast(F32),
                                        ALU.subtract).then_inc(xl_done, 1)

            def ffn_logit(T):
                dve.wait_ge(logits_ready, T + 1)
                L = bank[:, T_BANK, 0:NB * NEXP].rearrange("p (n e) -> p n e", n=NB)
                nc.vector.tensor_scalar(near0[:], L, -TINY, TINY, ALU.max, ALU.min).then_inc(route_step, 1)
                dve.wait_ge(route_step, ROUTE * T + 1)
                nc.vector.tensor_tensor(near0[:], near0[:], L, ALU.is_equal).then_inc(route_step, 1)
                dve.wait_ge(route_step, ROUTE * T + 2)
                nc.vector.scalar_tensor_tensor(logit[:], near0[:], 2 * TINY, L, ALU.mult, ALU.add).then_inc(route_step, 1)

            def ffn_score(T):
                r = ROUTE * T
                dve.wait_ge(route_step, r + 3)
                nc.vector.reciprocal(rlogit[:], logit[:]).then_inc(route_step, 1)
                dve.wait_ge(gsilu_done, T + 1)
                dve.wait_ge(route_step, r + 4)
                nc.vector.tensor_tensor(score[:], gsilu[:], rlogit[:], ALU.mult).then_inc(route_step, 1)
                dve.wait_ge(route_step, r + 5)
                nc.vector.tensor_tensor(biased[:, :, 0:NEXP], score[:],
                                        gb[:].rearrange("p (a e) -> p a e", a=1).to_broadcast([P, NB, NEXP]),
                                        ALU.add).then_inc(route_step, 1)

            def ffn_biased(T):
                dve.wait_ge(route_step, ROUTE * T + 6)

            def ffn_max(T):
                for n in range(NB):
                    ins = nc.vector.max(top8[:, n, :], biased[:, n, 0:NEXP])
                ins.then_inc(route_step, 1)
                dve.wait_ge(route_step, ROUTE * T + 7)
                nc.vector.tensor_copy(take[:, :, 0:TOPK], top8[:, :, 0:TOPK]).then_inc(route_step, 1)

            def ffn_take(T):
                dve.wait_ge(route_step, ROUTE * T + 8)

            def ffn_mark(T):
                r = ROUTE * T
                for n in range(NB):
                    ins = nc.vector.match_replace(marked[:, n, :], take[:, n, :], biased[:, n, :], TAKEN)
                ins.then_inc(route_step, 1)
                dve.wait_ge(route_step, r + 9)
                nc.vector.tensor_tensor(chosen[:], marked[:, :, 0:NEXP], biased[:, :, 0:NEXP],
                                        ALU.not_equal).then_inc(route_step, 1)

            def ffn_comb(T):
                r = ROUTE * T
                dve.wait_ge(route_step, r + 10)
                nc.vector.tensor_tensor(wsel[:], score[:], chosen[:], ALU.mult).then_inc(route_step, 1)
                dve.wait_ge(route_step, r + 11)
                nc.vector.reduce_sum(wsum[:], wsel[:], AX_X).then_inc(route_step, 1)
                dve.wait_ge(route_step, r + 12)
                nc.vector.reciprocal(rsum[:], wsum[:]).then_inc(route_step, 1)
                dve.wait_ge(route_step, r + 13)
                nc.vector.scalar_tensor_tensor(comb[:], wsel[:], ROUTE_SCALE,
                                               rsum[:].rearrange("p (n e) -> p n e", e=1).to_broadcast([P, NB, NEXP]),
                                               ALU.mult, ALU.mult).then_inc(route_step, 1)
                dve.wait_ge(route_step, r + 14)
                wait(dve, combT_ready, T)
                nc.vector.tensor_copy(comb_hl[:, :, 0:NEXP], comb[:]).then_inc(route_step, 1)
                dve.wait_ge(route_step, r + 15)
                nc.vector.tensor_tensor(comb_hl[:, :, NEXP:2 * NEXP], comb[:],
                                        comb_hl[:, :, 0:NEXP].bitcast(F32), ALU.subtract).then_inc(route_step, 1)

            def ffn_unit(T, q, j):
                g, c, k = (q + j) % 2, j % 2, j % 3
                dve.wait_ge(silu_done, UNITS * T + j + 1)
                if j < PAIRS:
                    dve.wait_ge(comb_ready, PAIRS * T + j + 1)
                    nc.vector.tensor_tensor(weighted[c][:], silu[g][:], bank[:, C_BANK[c], :],
                                            ALU.mult).then_inc(weighted_done, 1)
                    dve.wait_ge(weighted_done, PAIRS * T + j + 1)
                    dve.wait_ge(up_ready, PAIRS * T + j + 1)
                    wait(dve, down_done, UNITS * T + j - 2)
                    nc.vector.tensor_tensor(h[k][:], weighted[c][:], bank[:, U_BANK[c], :],
                                            ALU.mult).then_inc(h_done, 1)
                else:
                    wait(dve, down_done, UNITS * T + j - 2)
                    nc.vector.tensor_tensor(h[k][0:INTER, :], silu[g][0:INTER, :], bank[INTER:P, G_BANK[g], :],
                                            ALU.mult).then_inc(h_done, 1)

            def ffn_tile(T, Tx, q, first, last, loaded):
                def stats_next():
                    if loaded is not None:
                        dve.wait_ge(x_loaded[1 - q], loaded)
                    ln_stats(NB, NB * (Tx + 1), stats_done)

                def xn_next():
                    dve.wait_ge(rstd_done, T + 2)
                    dve.wait_ge(xnT_ready, T + 1)
                    ln_apply(NB, NB * (Tx + 1), xn_done)

                if not last:
                    stats_next()
                for j in range(UNITS):
                    if not last:
                        if j == 0:
                            dve.wait_ge(stats_done, T + 2)
                        elif j == 5:
                            ffn_biased(T + 1)
                        elif j == 6:
                            ffn_take(T + 1)
                    ffn_unit(T, q, j)
                    if not last:
                        if j == 0:
                            ln_mean_var(NB, T + 2, mv_done, var_done)
                        elif j == 1:
                            xn_next()
                        elif j == 2:
                            ffn_xl(T + 1, 1 - q)
                        elif j == 3:
                            ffn_logit(T + 1)
                        elif j == 4:
                            ffn_score(T + 1)
                        elif j == 5:
                            ffn_max(T + 1)
                        elif j == 6:
                            ffn_mark(T + 1)
                            ffn_comb(T + 1)
                    if j == 6 and not first:
                        residual(T - 1, Tx - 1)

            def residual(T, Tx):
                dve.wait_ge(y_ready, T + 1)
                xt = X[:, tile_blocks(Tx), :]
                nc.vector.scalar_tensor_tensor(xt, bank[:, T_BANK, :].rearrange("p (n d) -> p n d", n=NB), 0.5, xt,
                                               ALU.mult, ALU.add).then_inc(x_done, 1)

            def ffn(base):
                load = base == 0
                if load:
                    dve.wait_ge(x_loaded[0], 16)
                ln_stats(NB, 0, stats_done)
                dve.wait_ge(stats_done, base + 1)
                ln_mean_var(NB, base + 1, mv_done, var_done)
                dve.wait_ge(rstd_done, base + 1)
                ln_apply(NB, 0, xn_done)
                ffn_xl(base, 0)
                ffn_logit(base)
                ffn_score(base)
                ffn_biased(base)
                ffn_max(base)
                ffn_take(base)
                ffn_mark(base)
                ffn_comb(base)
                ffn_tile(base, 0, 0, True, False, 16 if load else None)
                with dve.Fori(0, TILES // 2 - 1) as k:
                    ffn_tile(base + 2 * k + 1, 2 * k + 1, 1, False, False, 16 * (k + 2) if load else None)
                    ffn_tile(base + 2 * k + 2, 2 * k + 2, 0, False, False, 16 * (k + 2) if load else None)
                ffn_tile(base + TILES - 1, TILES - 1, 1, False, True, None)
                residual(base + TILES - 1, TILES - 1)

            def attn_item(item, b, p):
                kind, n = item
                if kind == "xnT":
                    dve.wait_ge(a_xh_done, 2 * b + n + 1)
                    nc.vector.tensor_tensor(xl[n][:], bank[:, M_BANK, :], xh[n][:].bitcast(F32),
                                            ALU.subtract).then_inc(a_xl_done, 1)
                elif kind == "qkv":
                    s = n % 2
                    dve.wait_ge(qkv_done, QB * b + n + 1)
                    if n >= 2:
                        dve.wait_ge(rot_done, QB * b + n - 1)
                    else:
                        wait(dve, rot_done, QB * (b - 1) + QB + n - 1)
                    nc.vector.tensor_tensor(rope_c[s][:], qkv[p][:, n, 0:2 * D].rearrange("p (w d) -> p w d", w=2),
                                            cos[:, n:n + 1, :].to_broadcast([P, 2, D]), ALU.mult).then_inc(rope_c_done, 1)
                else:
                    dve.wait_ge(qkT_h_done, QB // 2 * b + n + 1)
                    cols = slice(2 * P * n, 2 * P * (n + 1))
                    nc.vector.tensor_tensor(qkT_l[p][:, :, cols], bank[:, M_BANK, :].rearrange("p (w c) -> p w c", w=2),
                                            qkT_h[p][:, :, cols].bitcast(F32), ALU.subtract).then_inc(qkT_l_done, 1)

            def attn_max(b, i):
                s, w = i % 2, (i + 1) * P
                dve.wait_ge(scores_ready, QB * b + i + 1)
                nc.vector.reduce_max(rowmax[s][:], bank[:, 2 * s:2 * s + 2, :].rearrange("p a c -> p (a c)")[:, 0:w],
                                     AX_X).then_inc(rowmax_done, 1)
                dve.wait_ge(rowmax_done, QB * b + i + 1)
                wait(dve, exp_done, QB * b + i - 1)
                nc.vector.tensor_scalar_mul(negmax[s][:], rowmax[s][:], -SCORE_SCALE).then_inc(negmax_done, 1)

            def attn_residual(b, p, i):
                dve.wait_ge(exp_done, QB * b + i + 1)
                nc.vector.reciprocal(rrow[p][:, i:i + 1], rowsum[p][:, i:i + 1]).then_inc(rrow_done, 1)
                dve.wait_ge(rrow_done, QB * b + i + 1)
                dve.wait_ge(pv_ready, QB * b + i + 1)
                xb = X[:, bass.ds(QB * b + i, 1), :].rearrange("p a d -> p (a d)")
                nc.vector.scalar_tensor_tensor(xb, bank[:, O_BANK, 0:D], rrow[p][:, i:i + 1], xb,
                                               ALU.mult, ALU.add).then_inc(attn_done, 1)

            def attn_mean_var(b):
                ln_mean_var(QB, b + 1, a_mv_done, a_var_done)

            def attn_xn(b):
                dve.wait_ge(a_rstd_done, b + 1)
                wait(dve, a_xnT_ready, 2 * b)
                ln_apply(QB, QB * b, a_xn_done)

            def attn_batch(b, p, first, last):
                for i in range(QB):
                    if i == 0 and not last:
                        ln_stats(QB, QB * (b + 1), a_stats_done)
                        dve.wait_ge(a_stats_done, b + 2)
                    if i + 1 < QB:
                        attn_max(b, i + 1)
                    elif not last:
                        attn_max(b + 1, 0)
                    if i >= 1:
                        attn_residual(b, p, i - 1)
                    elif not first:
                        attn_residual(b - 1, 1 - p, QB - 1)
                    if not last:
                        if i == 0:
                            attn_mean_var(b + 1)
                            attn_xn(b + 1)
                        else:
                            attn_item(prep_item(i, 0), b + 1, 1 - p)
                            attn_item(prep_item(i, 1), b + 1, 1 - p)

            ffn(0)
            dve.wait_ge(x_done, TILES)
            ln_stats(QB, 0, a_stats_done)
            dve.wait_ge(a_stats_done, 1)
            attn_mean_var(0)
            attn_xn(0)
            for item in PREP_ITEMS:
                attn_item(item, 0, 0)
            attn_max(0, 0)
            attn_batch(0, 0, True, False)
            with dve.Fori(0, B // 2 - 1) as k:
                attn_batch(2 * k + 1, 1, False, False)
                attn_batch(2 * k + 2, 0, False, False)
            attn_batch(B - 1, 1, False, True)
            attn_residual(B - 1, 1, QB - 1)
            dve.wait_ge(attn_done, B * QB)
            ffn(TILES)

        @block.tensor
        def _(pe):
            def mm(dst, lhsT, rhs, start, stop):
                return nc.tensor.matmul(dst, lhsT, rhs, start=start, stop=stop)

            def mm3(dst, lh, ll, rh, rl, start=True, stop=True):
                mm(dst, lh, rh, start, False)
                mm(dst, lh, rl, False, False)
                return mm(dst, ll, rh, False, stop)

            def ffn_xnT(T):
                pe.wait_ge(xn_done, T + 1)
                wait(pe, combT_done, T)
                for n in range(NB):
                    ins = nc.tensor.transpose(bank[:, T_BANK, n * P:(n + 1) * P], xn[:, n, :], ident[:])
                ins.then_inc(xnT_ready, 1)

            def ffn_logits(T, q):
                pe.wait_ge(xl_done, T + 1)
                for n in range(NB):
                    blk = slice(n * P, (n + 1) * P)
                    ins = mm3(bank[:, T_BANK, n * NEXP:(n + 1) * NEXP], xh[q][:, blk], xl[q][:, blk], gw_h[:], gw_l[:])
                ins.then_inc(logits_ready, 1)

            def ffn_combT(T):
                pe.wait_ge(route_step, ROUTE * (T + 1))
                for n in range(NB):
                    ins = nc.tensor.transpose(bank[:, T_BANK, n * P:(n + 1) * P], comb_hl[:, n, :].bitcast(F32), ident[:])
                ins.then_inc(combT_ready, 1)

            def ffn_y(T):
                pe.wait_ge(yT_done, T + 1)
                for n in range(NB):
                    ins = nc.tensor.transpose(bank[:, T_BANK, n * P:(n + 1) * P], yT[:, n * P:(n + 1) * P], ident[:])
                ins.then_inc(y_ready, 1)

            def ffn_up(T, q, j):
                g, c = (q + j) % 2, j % 2
                if j == 1:
                    wait(pe, h_done, UNITS * T)
                else:
                    wait(pe, silu_done, UNITS * T + j - 1)
                mm3(bank[:, G_BANK[g], :], w13_h[:, 2 * j, :], w13_l[:, 2 * j, :], xh[q][:], xl[q][:]).then_inc(gate_ready, 1)
                if j < PAIRS:
                    wait(pe, weighted_done, PAIRS * T + j - 1)
                    if j == 0:
                        pe.wait_ge(combT_done, T + 1)
                    mm(bank[:, C_BANK[c], :], sel[:, j, :], combT[q][:], True, True).then_inc(comb_ready, 1)
                    if j >= 2:
                        pe.wait_ge(h_done, UNITS * T + j - 1)
                    else:
                        wait(pe, h_done, UNITS * (T - 1) + PAIRS - 1 + j)
                    mm3(bank[:, U_BANK[c], :], w13_h[:, 2 * j + 1, :], w13_l[:, 2 * j + 1, :],
                        xh[q][:], xl[q][:]).then_inc(up_ready, 1)

            def ffn_down(T, j):
                pe.wait_ge(h_done, UNITS * T + j + 1)
                if j == 0:
                    wait(pe, yT_done, T)
                mm(bank[:, Y_BANK, :], w2[:, j, :], h[j % 3][:], j == 0, j == UNITS - 1).then_inc(down_done, 1)

            def ffn_tile(T, q, first, last):
                for j in range(UNITS):
                    ffn_up(T, q, j)
                    if j >= 2:
                        ffn_down(T, j - 2)
                    elif not first:
                        ffn_down(T - 1, UNITS - 2 + j)
                    if j == 2 and not last:
                        ffn_xnT(T + 1)
                    if j == 3 and not last:
                        ffn_logits(T + 1, 1 - q)
                    if j == 5 and not first:
                        if last:
                            pe.wait_ge(combT_done, T + 1)
                        else:
                            pe.wait_ge(route_step, ROUTE * (T + 1) + 3)
                        ffn_y(T - 1)
                    if j == UNITS - 1 and not last:
                        wait(pe, x_done, T)
                        ffn_combT(T + 1)

            def ffn(base):
                ffn_xnT(base)
                ffn_logits(base, 0)
                ffn_combT(base)
                ffn_tile(base, 0, True, False)
                with pe.Fori(0, TILES // 2 - 1) as k:
                    ffn_tile(base + 2 * k + 1, 1, False, False)
                    ffn_tile(base + 2 * k + 2, 0, False, False)
                T = base + TILES - 1
                ffn_tile(T, 1, False, True)
                ffn_down(T, UNITS - 2)
                ffn_down(T, UNITS - 1)
                pe.wait_ge(x_done, T)
                ffn_y(T)

            def attn_item(item, b, p):
                kind, n = item
                if kind == "xnT":
                    if n == 0:
                        pe.wait_ge(a_xn_done, b + 1)
                        wait(pe, qkT_l_done, QB // 2 * b)
                    else:
                        pe.wait_ge(a_xl_done, 2 * b + 1)
                    for m in range(NB):
                        ins = nc.tensor.transpose(bank[:, M_BANK, m * P:(m + 1) * P], xn[:, NB * n + m, :], ident[:])
                    ins.then_inc(a_xnT_ready, 1)
                elif kind == "qkv":
                    a, blk = n // NB, slice(n % NB * P, (n % NB + 1) * P)
                    if n == 0:
                        pe.wait_ge(a_xl_done, 2 * b + 2)
                    else:
                        pe.wait_ge(qkv_done, QB * b + n)
                        before = PREP_ITEMS[PREP_ITEMS.index(item) - 1]
                        if before[0] == "qkT":
                            pe.wait_ge(qkT_l_done, QB // 2 * b + before[1] + 1)
                    mm3(bank[:, M_BANK, 0:3 * D], xh[a][:, blk], xl[a][:, blk], wqkv_h[:], wqkv_l[:]).then_inc(qkv_ready, 1)
                else:
                    pe.wait_ge(rot_done, QB * b + 2 * n + 2)
                    before = PREP_ITEMS[PREP_ITEMS.index(item) - 1]
                    pe.wait_ge(qkv_done, QB * b + before[1] + 1)
                    for m in range(2):
                        for w in range(2):
                            at = w * 2 * P + m * P
                            ins = nc.tensor.transpose(bank[:, M_BANK, at:at + P], rot[m][:, w, :], ident[:])
                    ins.then_inc(qkT_ready, 1)

            def attn_scores(b, p, i):
                s = i % 2
                pe.wait_ge(qkT_l_done, QB // 2 * b + i // 2 + 1)
                wait(pe, exp_done, QB * b + i - 1)
                qs = slice(i * P, (i + 1) * P)
                for c in range(1 + i // 4):
                    k0, k1 = 512 * c, min(512 * (c + 1), (i + 1) * P)
                    dst = bank[:, 2 * s + c, 0:k1 - k0]
                    diag = c == i // 4
                    ins = mm3(dst, qkT_h[p][:, 0, qs], qkT_l[p][:, 0, qs], qkT_h[p][:, 1, k0:k1], qkT_l[p][:, 1, k0:k1],
                              True, not diag)
                    if diag:
                        ins = mm(bank[:, 2 * s + c, k1 - k0 - P:k1 - k0], ident_r[:], mask[:], False, True)
                ins.then_inc(scores_ready, 1)

            def attn_probT(b, i, c):
                s, m = i % 2, chunk_index(i, c)
                if c == 0:
                    pe.wait_ge(exp_done, QB * b + i + 1)
                wait(pe, probT_done, PT_CHUNKS * b + m - 1)
                blocks = min(4, i + 1 - 4 * c)
                for a in range(blocks):
                    k0 = (4 * c + a) * P
                    ins = nc.tensor.transpose(bank[:, PT_BANK[m % 2], a * P:(a + 1) * P], prob[s][:, k0:k0 + P], ident[:])
                ins.then_inc(probT_ready, 1)

            def attn_pv(b, p, i):
                s = i % 2
                wait(pe, attn_done, QB * b + i)
                for kb in range(i + 1):
                    if kb % 4 == 0:
                        pe.wait_ge(probT_done, PT_CHUNKS * b + chunk_index(i, kb // 4) + 1)
                    ins = mm(bank[:, O_BANK, 0:D], probT[s][:, kb, :], qkv[p][:, kb, 2 * D:3 * D], kb == 0, kb == i)
                ins.then_inc(pv_ready, 1)

            def attn_batch(b, p, last):
                for i in range(QB):
                    if i + 1 < QB:
                        attn_scores(b, p, i + 1)
                    elif not last:
                        attn_scores(b + 1, 1 - p, 0)
                    if not last and i >= 1:
                        attn_item(prep_item(i, 0), b + 1, 1 - p)
                    for c in range(1 + i // 4):
                        attn_probT(b, i, c)
                    if not last and i >= 1:
                        attn_item(prep_item(i, 1), b + 1, 1 - p)
                    attn_pv(b, p, i)

            pe.wait_ge(weights_loaded, 16 * WEIGHT_LOADS)
            pe.wait_ge(hi_set, 6)
            pe.wait_ge(weights_split, SPLITS)
            ffn(0)
            pe.wait_ge(x_done, TILES)
            for item in PREP_ITEMS:
                attn_item(item, 0, 0)
            attn_scores(0, 0, 0)
            attn_batch(0, 0, False)
            with pe.Fori(0, B // 2 - 1) as k:
                attn_batch(2 * k + 1, 1, False)
                attn_batch(2 * k + 2, 0, False)
            attn_batch(B - 1, 1, True)
            pe.wait_ge(attn_done, B * QB)
            ffn(TILES)


def chunk_index(i, c):
    c = min(c, i // 4)
    return i if i < 4 else 4 + 2 * (i - 4) + c


def rope_tables():
    f = np.float32
    i = np.arange(D // 2, dtype=f)
    theta = np.power(f(10000.0), (f(-2.0) * (i - f(1.0)) / f(D)).astype(f)).astype(f)
    ang = (np.arange(M, dtype=f)[:, None] * theta[None, :]).astype(f).astype(np.float64)
    c = np.repeat(np.cos(ang).astype(f), 2, axis=1)
    s = np.repeat(np.sin(ang).astype(f), 2, axis=1)
    s[:, 1::2] *= -1
    return [np.ascontiguousarray(t.reshape(QB, P, D).transpose(1, 0, 2)) for t in (c, s)]


def kernel(**inputs):
    import concourse.bacc as bacc
    from concourse.bass_utils import run_bass_kernel_spmd

    a = {k: np.asarray(v) for k, v in inputs.items()}
    w13 = a["L0_ffn_w13"].reshape(PAIRS, 2, 2, INTER, D).transpose(4, 0, 2, 1, 3).reshape(D, 2 * PAIRS, P)
    w13T = np.concatenate([w13, a["L0_ffn_w13_s"].T.reshape(D, 1, P)], axis=1)
    w2 = a["L0_ffn_w2"].reshape(PAIRS, 2, D, INTER).transpose(1, 3, 0, 2).reshape(P, PAIRS, D)
    w2s = np.concatenate([a["L0_ffn_w2_s"].T, np.zeros((P - INTER, D), np.float32)], axis=0)
    w2T = np.concatenate([w2, w2s.reshape(P, 1, D)], axis=1)
    wqkvT = np.concatenate([a["L0_attn_w_q"].T, a["L0_attn_w_k"].T, a["L0_attn_w_v"].T], axis=1)
    sel = np.zeros((P, PAIRS, P), np.float32)
    for e in range(NEXP):
        sel[[e, NEXP + e], e // 2, e % 2 * INTER:(e % 2 + 1) * INTER] = 1.0
    row, col = np.arange(P)[:, None], np.arange(P)[None, :]
    mask = np.where(col > row, np.float32(MASKED), np.float32(0.0)).astype(np.float32)
    cos, sin = rope_tables()
    arrays = {
        "x": a["L0_attn_x"], "w13T": w13T, "w2T": w2T, "wqkvT": wqkvT, "gwT": a["L0_ffn_gate_w"].T,
        "gate_b": np.tile(a["L0_ffn_gate_b"].reshape(1, NEXP), (P, 1)),
        "ident": np.eye(P, dtype=np.float32), "sel": sel, "mask": mask, "cos": cos, "sin": sin,
    }
    arrays = {f"in_{k}": np.ascontiguousarray(v) for k, v in arrays.items()}
    nc = bacc.Bacc("TRN2", target_bir_lowering=False, num_devices=1)
    args = [nc.dram_tensor(k, v.shape, mybir.dt.from_np(v.dtype), kind="ExternalInput").ap() for k, v in arrays.items()]
    args.append(nc.dram_tensor("out_x", (B, M, D), F32, kind="ExternalOutput").ap())
    macaron(nc, *args)
    r = run_bass_kernel_spmd(nc, [arrays], core_ids=[0])
    return r.results[0]["out_x"]
```

```python
from contextlib import ExitStack

import numpy as np

import concourse.bass as bass
from concourse import mybir

P = 128
B, M, D = 8, 1024, 128
INTER, NEXP, TOPK = 64, 16, 4
ROUTE_SCALE = 2.5
EPS = 1e-5
TILE = 512
NB = TILE // P
TILES = B * M // TILE
PAIRS = NEXP * INTER // P
UNITS = PAIRS + 1
QB = M // P
SCORE_SCALE = float(1.0 / np.sqrt(np.float32(D)))
MASKED = -3.0e38
SENTINEL, TAKEN = -3.0e38, 3.0e38
TINY = 1.0e-30
ROUTE = 15
PT_CHUNKS = 12

F32 = mybir.dt.float32
F32R = mybir.dt.float32r
ALU = mybir.AluOpType
ACT = mybir.ActivationFunctionType
AX_X = mybir.AxisListType.X

G_BANK, U_BANK, YT_BANK, Y_BANK, T_BANK = (0, 1), (2, 3), 4, (5, 6), 7
PT_BANK, O_BANK, M_BANK = 4, 6, (5, 7)

STEP_ITEMS = [[("xnT", 0), ("xnT", 1)], [("qkv", 0), ("qkv", 1), ("qkv", 2)], [("qkv", 3), ("qkT", 0), ("qkv", 4)],
              [("qkv", 5), ("qkT", 1)], [("qkv", 6), ("qkv", 7)], [("qkT", 2)], [("qkT", 3)], []]
ITEMS = [item for step in STEP_ITEMS for item in step]
ROPE_BUFS = 4
LAG = 3
EARLY = 2
COMB_LOADS = 2


def macaron(nc, x, w13T, w2T, wqkvT, gwT, gate_b, ident_d, mask_d, cos_d, sin_d, comb_d, out):
    x_v = x.rearrange("b (n p) d -> p (b n) d", p=P)
    out_v = out.rearrange("b (n p) d -> p (b n) d", p=P)

    with ExitStack() as ctx:
        def sb(name, shape, dt=F32):
            return ctx.enter_context(nc.sbuf_tensor(name, shape, dt))

        def sem(name):
            return ctx.enter_context(nc.semaphore(name))

        bank = ctx.enter_context(nc.psum_tensor("bank", [P, 8, 512], F32))

        X = sb("X", [P, (B + 1) * QB, D])
        ident = sb("ident", [P, P])
        w13_h = sb("w13_h", [P, UNITS * 2 - 1, P], F32R)
        w13_l = sb("w13_l", [P, UNITS * 2 - 1, P], F32R)
        w2_h = sb("w2_h", [P, UNITS, D], F32R)
        w2_l = sb("w2_l", [P, UNITS, D], F32R)
        wqkv_h = sb("wqkv_h", [P, 3 * D], F32R)
        wqkv_l = sb("wqkv_l", [P, 3 * D], F32R)
        gw_f = sb("gw_f", [P, NEXP])
        gw_hl = sb("gw_hl", [P, 2 * NEXP], F32R)
        gb = sb("gb", [P, NEXP])
        mask = sb("mask", [P, P], F32R)
        ident_r = sb("ident_r", [P, P], F32R)
        cos = sb("cos", [P, QB, 2, D])
        sin = sb("sin", [P, QB, 2, D])
        neg_half = sb("neg_half", [P, QB])

        stats = sb("stats", [P, QB, 6])
        mv = sb("mv", [P, QB, 2])
        var_eps = sb("var_eps", [P, QB])
        rstd = sb("rstd", [P, QB])
        neg_one = sb("neg_one", [P, NB])
        neg_mean = sb("neg_mean", [P, NB])
        neg_shift = sb("neg_shift", [P, NB])
        xn = sb("xn", [P, QB, D])
        xh = [sb(f"xh{q}", [P, TILE], F32R) for q in range(2)]
        xl = [sb(f"xl{q}", [P, TILE], F32R) for q in range(2)]

        logit0 = sb("logit0", [P, NB, NEXP])
        near0 = sb("near0", [P, NB, NEXP])
        logit = sb("logit", [P, NB, NEXP])
        gsilu = sb("gsilu", [P, NB, NEXP])
        rlogit = sb("rlogit", [P, NB, NEXP])
        score = sb("score", [P, NB, NEXP])
        biased = sb("biased", [P, NB, NEXP + TOPK])
        top8 = sb("top8", [P, NB, 8])
        take = sb("take", [P, NB, 8])
        marked = sb("marked", [P, NB, NEXP + TOPK])
        chosen = sb("chosen", [P, NB, NEXP])
        wsel = sb("wsel", [P, NB, NEXP])
        wsum = sb("wsum", [P, NB])
        rsum = sb("rsum", [P, NB])
        comb = sb("comb", [P, NB, NEXP])
        combT = [sb(f"combT{q}", [NEXP, TILE]) for q in range(2)]

        h_h = [sb(f"h_h{k}", [P, TILE], F32R) for k in range(3)]
        h_l = [sb(f"h_l{k}", [P, TILE], F32R) for k in range(3)]

        qkv_both = sb("qkv_both", [P, 2, QB, 3 * D])
        qkv = [qkv_both[:, p, :, :] for p in range(2)]
        rope_c = [sb(f"rope_c{p}", [P, 2, D]) for p in range(ROPE_BUFS)]
        rope_s = [sb(f"rope_s{p}", [P, 2, D]) for p in range(ROPE_BUFS)]
        rot = [sb(f"rot{p}", [P, 2, D]) for p in range(ROPE_BUFS)]
        qkT = [sb(f"qkT{p}", [P, 2, 2, M], F32R) for p in range(2)]
        qkT_h = [qkT[p][:, 0, :, :] for p in range(2)]
        qkT_l = [qkT[p][:, 1, :, :] for p in range(2)]
        negmax = [sb(f"negmax{p}", [P, 1]) for p in range(2)]
        rowsum = [sb(f"rowsum{p}", [P, QB]) for p in range(2)]
        rrow = [sb(f"rrow{p}", [P, QB]) for p in range(2)]
        prob = [sb(f"prob{p}", [P, M]) for p in range(2)]
        probT = [sb(f"probT{p}", [P, QB, P]) for p in range(2)]

        comb_b = [qkT[q][:].bitcast(F32).rearrange("p a w m -> p (a w m)").rearrange("p (j t) -> p j t", t=TILE)
                  for q in range(2)]
        silu = [prob[q][:, 0:TILE] for q in range(2)]
        weighted = [prob[q][:, TILE:2 * TILE] for q in range(2)]
        h = [probT[q][:, 0:NB, :].rearrange("p a c -> p (a c)") for q in range(2)]
        yT = probT[0][:, NB:2 * NB, :].rearrange("p a c -> p (a c)")

        staged = qkv_both[:].rearrange("p a n d -> p (a n d)").rearrange("p (n c) -> p n c", c=P)
        parts, at = {}, 0
        for name, blocks in (("w13", 2 * UNITS - 1), ("w2", UNITS), ("wqkv", 3), ("mask", 1)):
            parts[name] = staged[:, at:at + blocks, :]
            at += blocks
        w13_f, w2_f = parts["w13"], parts["w2"]
        wqkv_f, mask_f = (parts[n].rearrange("p n c -> p (n c)") for n in ("wqkv", "mask"))

        x_loaded = [sem(f"x_loaded{n}") for n in range(3)]
        gate_loaded = sem("gate_loaded")
        w13_loaded = [sem(f"w13_loaded{n}") for n in range(2)]
        w2_loaded = sem("w2_loaded")
        attn_loaded = sem("attn_loaded")
        consts_set = sem("consts_set")
        gw_hi = sem("gw_hi")
        w13_hi = [sem(f"w13_hi{n}") for n in range(2)]
        w2_hi = sem("w2_hi")
        wqkv_hi = sem("wqkv_hi")
        consts_rounded = sem("consts_rounded")
        gw_split = sem("gw_split")
        w13_split = [sem(f"w13_split{n}") for n in range(2)]
        w2_split = sem("w2_split")
        wqkv_split = sem("wqkv_split")
        stats_done = sem("stats_done")
        mv_done = sem("mv_done")
        var_done = sem("var_done")
        rstd_done = sem("rstd_done")
        neg_mean_done = sem("neg_mean_done")
        neg_shift_done = sem("neg_shift_done")
        xn_done = sem("xn_done")
        xnT_ready = sem("xnT_ready")
        xh_done = sem("xh_done")
        xl_done = sem("xl_done")
        logits_ready = sem("logits_ready")
        gsilu_done = sem("gsilu_done")
        route_step = sem("route_step")
        combT_ready = sem("combT_ready")
        combT_done = sem("combT_done")
        gate_ready = sem("gate_ready")
        comb_written = sem("comb_written")
        comb_loaded = [sem(f"comb_loaded{n}") for n in range(COMB_LOADS)]
        up_ready = sem("up_ready")
        silu_done = sem("silu_done")
        weighted_done = sem("weighted_done")
        h_done = sem("h_done")
        h_hi_done = sem("h_hi_done")
        h_lo_done = sem("h_lo_done")
        down_done = sem("down_done")
        yT_done = sem("yT_done")
        y_ready = sem("y_ready")
        x_done = sem("x_done")
        stored = sem("stored")
        a_stats_done = sem("a_stats_done")
        a_mv_done = sem("a_mv_done")
        a_var_done = sem("a_var_done")
        a_rstd_done = sem("a_rstd_done")
        a_xn_done = sem("a_xn_done")
        a_xnT_ready = sem("a_xnT_ready")
        a_xh_done = sem("a_xh_done")
        a_xl_done = sem("a_xl_done")
        qkv_ready = sem("qkv_ready")
        qkv_done = sem("qkv_done")
        rope_c_done = sem("rope_c_done")
        rope_s_done = sem("rope_s_done")
        rot_done = sem("rot_done")
        qkT_ready = sem("qkT_ready")
        qkT_h_done = sem("qkT_h_done")
        qkT_l_done = sem("qkT_l_done")
        scores_ready = sem("scores_ready")
        negmax_done = sem("negmax_done")
        exp_done = sem("exp_done")
        probT_ready = sem("probT_ready")
        probT_done = sem("probT_done")
        pv_ready = sem("pv_ready")
        rrow_done = sem("rrow_done")
        attn_done = sem("attn_done")

        early = slice(0, 2 * EARLY), slice(2 * EARLY, 2 * UNITS - 1)

        def wait(eng, s, n):
            if not isinstance(n, int) or n > 0:
                eng.wait_ge(s, n)

        def tile_blocks(T):
            return bass.ds(NB * T, NB)

        def ln_count(T):
            return T + 1 + ln_count.phase

        def ffn_phase(base):
            ln_count.phase = base // TILES

        block = ctx.enter_context(nc.Block())

        @block.sync
        def _(sp):
            def load(dst, src, s):
                sp.dma_start(dst, src).then_inc(s, 16)

            load(X[:, 0:NB, :], x_v[:, 0:NB, :], x_loaded[0])
            load(ident[:], ident_d, gate_loaded)
            load(gw_f[:], gwT, gate_loaded)
            load(gb[:], gate_b, gate_loaded)
            load(w13_f[:, early[0], :], w13T[:, early[0], :], w13_loaded[0])
            load(w13_f[:, early[1], :], w13T[:, early[1], :], w13_loaded[1])
            load(X[:, NB:3 * NB, :], x_v[:, NB:3 * NB, :], x_loaded[1])
            load(w2_f, w2T, w2_loaded)
            load(X[:, 3 * NB:B * QB, :], x_v[:, 3 * NB:, :], x_loaded[2])

            def comb_rows(T, q):
                sp.wait_ge(combT_done, T + 1)
                sp.dma_start(comb_d[q], combT[q][:]).then_inc(comb_written, 16)
                sp.wait_ge(comb_written, 16 * (T + 1))
                src = comb_d[q].rearrange("(j a) t -> a j t", a=2)
                n = PAIRS // COMB_LOADS
                for g in range(COMB_LOADS):
                    for a in range(2):
                        sp.dma_start(comb_b[q][a * INTER:(a + 1) * INTER, n * g:n * (g + 1), :],
                                     src[a:a + 1, n * g:n * (g + 1), :].to_broadcast([INTER, n, TILE])
                                     ).then_inc(comb_loaded[g], 16)

            def store(t):
                sp.wait_ge(x_done, TILES + 1 + t)
                sp.dma_start(out_v[:, tile_blocks(t), :], X[:, tile_blocks(t), :]).then_inc(stored, 16)

            def ffn(base, stores):
                comb_rows(base, 0)
                if stores:
                    sp.wait_ge(scores_ready, B * QB)
                else:
                    load(wqkv_f, wqkvT, attn_loaded)
                    load(mask_f, mask_d, attn_loaded)
                    load(cos[:], cos_d, attn_loaded)
                    load(sin[:], sin_d, attn_loaded)
                comb_rows(base + 1, 1)
                with sp.Fori(0, TILES // 2 - 1) as k:
                    for q in range(2):
                        comb_rows(base + 2 * k + 2 + q, q)
                        if stores:
                            store(2 * k + q)
                if stores:
                    store(TILES - 2)
                    store(TILES - 1)

            ffn(0, False)
            sp.wait_ge(scores_ready, (B - 1) * QB)
            ffn(TILES, True)
            sp.wait_ge(stored, 16 * TILES)

        @block.gpsimd
        def _(pool):
            nc.gpsimd.memset(neg_half[:], -0.5).then_inc(consts_set, 1)
            nc.gpsimd.memset(neg_one[:], -1.0).then_inc(consts_set, 1)
            nc.gpsimd.memset(take[:], SENTINEL).then_inc(consts_set, 1)
            nc.gpsimd.memset(biased[:], SENTINEL).then_inc(consts_set, 1)
            nc.gpsimd.memset(X[:, B * QB:, :], 0.0).then_inc(consts_set, 1)
            pool.wait_ge(consts_set, 2)

            def low_half(lo, f, hi, done):
                nc.gpsimd.tensor_tensor(lo, f, hi.bitcast(F32), ALU.subtract).then_inc(done, 1)

            def ffn_rstd(T):
                pool.wait_ge(var_done, ln_count(T))
                nc.gpsimd.tensor_tensor(neg_mean[:], mv[:, 0:NB, 0], neg_one[:], ALU.mult).then_inc(neg_mean_done, 1)
                nc.gpsimd.tensor_tensor(rstd[:, 0:NB], var_eps[:, 0:NB], neg_half[:, 0:NB],
                                        ALU.pow).then_inc(rstd_done, 1)
                pool.wait_ge(neg_mean_done, ln_count(T))
                pool.wait_ge(rstd_done, ln_count(T))
                nc.gpsimd.tensor_tensor(neg_shift[:], neg_mean[:], rstd[:, 0:NB], ALU.mult).then_inc(neg_shift_done, 1)

            def ffn_tile(T, q, last):
                for j in range(UNITS):
                    g, k = (q + j) % 2, j % 3
                    if j == 0:
                        wait(pool, h_lo_done, UNITS * T)
                    elif j == PAIRS:
                        pool.wait_ge(h_lo_done, UNITS * T + j)
                    pool.wait_ge(h_hi_done, UNITS * T + j + 1)
                    if j < PAIRS:
                        low_half(h_l[k][:], h[g], h_h[k][:], h_lo_done)
                    else:
                        low_half(h_h[k][INTER:P, :], h[g][0:INTER, :], h_h[k][0:INTER, :], h_lo_done)
                    if j == 5 and not last:
                        ffn_rstd(T + 2)

            def ffn(base):
                ffn_phase(base)
                ffn_rstd(base)
                ffn_rstd(base + 1)
                if base == 0:
                    pool.wait_ge(w13_hi[1], 1)
                    low_half(w13_l[:, early[1], :], w13_f[:, early[1], :], w13_h[:, early[1], :], w13_split[1])
                    pool.wait_ge(w2_hi, 1)
                    low_half(w2_l[:], w2_f, w2_h[:], w2_split)
                ffn_tile(base, 0, False)
                if base == 0:
                    pool.wait_ge(h_lo_done, UNITS)
                    pool.wait_ge(wqkv_hi, 1)
                    low_half(wqkv_l[:], wqkv_f, wqkv_h[:], wqkv_split)
                with pool.Fori(0, TILES // 2 - 1) as k:
                    ffn_tile(base + 2 * k + 1, 1, False)
                    ffn_tile(base + 2 * k + 2, 0, False)
                ffn_tile(base + TILES - 1, 1, True)
                pool.wait_ge(h_lo_done, UNITS * (base + TILES))

            def attn_rstd(b):
                pool.wait_ge(a_var_done, b + 1)
                nc.gpsimd.tensor_tensor(rstd[:], var_eps[:], neg_half[:], ALU.pow).then_inc(a_rstd_done, 1)

            def rope(b, p, n):
                s = n % ROPE_BUFS
                pool.wait_ge(qkv_done, QB * b + n + 1)
                src = qkv[p][:, n, 0:2 * D].rearrange("p (w i e) -> p w i e", w=2, e=2)[:, :, :, ::-1]
                nc.gpsimd.tensor_tensor(rope_s[s][:].rearrange("p w (i e) -> p w i e", e=2), src,
                                        sin[:, n, :, :].rearrange("p w (i e) -> p w i e", e=2),
                                        ALU.mult).then_inc(rope_s_done, 1)
                pool.wait_ge(rope_s_done, QB * b + n + 1)
                pool.wait_ge(rope_c_done, QB * b + n + 1)
                wait(pool, qkT_ready, QB // 2 * b + (n - ROPE_BUFS) // 2 + 1)
                nc.gpsimd.tensor_tensor(rot[s][:], rope_c[s][:], rope_s[s][:], ALU.add).then_inc(rot_done, 1)

            def attn_prep(b, p):
                for n in range(QB):
                    rope(b, p, n)
                attn_rstd(b + 1)

            ffn(0)
            pool.wait_ge(attn_loaded, 16 * 4)
            attn_rstd(0)
            attn_prep(0, 0)
            with pool.Fori(0, B // 2 - 1) as k:
                attn_prep(2 * k + 1, 1)
                attn_prep(2 * k + 2, 0)
            attn_prep(B - 1, 1)
            ffn(TILES)

        @block.scalar
        def _(act):
            def copy(dst, src):
                return nc.scalar.activation(dst, src, ACT.Copy)

            def ffn_xn(T, Tx):
                act.wait_ge(neg_shift_done, ln_count(T))
                wait(act, xnT_ready, T)
                for n in range(NB):
                    ins = nc.scalar.activation(xn[:, n, :], X[:, bass.ds(NB * Tx + n, 1), :].rearrange("p a d -> p (a d)"),
                                               ACT.Identity, bias=neg_shift[:, n:n + 1], scale=rstd[:, n:n + 1])
                ins.then_inc(xn_done, 1)

            def ffn_xh(T, q):
                act.wait_ge(xnT_ready, T + 1)
                copy(xh[q][:], bank[:, T_BANK, :]).then_inc(xh_done, 1)

            def ffn_gsilu(T):
                act.wait_ge(route_step, ROUTE * T + 4)
                nc.scalar.activation(gsilu[:], logit[:], ACT.Silu).then_inc(gsilu_done, 1)

            def ffn_combT(T, q):
                act.wait_ge(combT_ready, T + 1)
                wait(act, comb_written, 16 * (T - 1))
                copy(combT[q][:], bank[0:NEXP, T_BANK, :]).then_inc(combT_done, 1)

            def ffn_silu(T, q, j):
                g = (q + j) % 2
                rows = P if j < PAIRS else INTER
                act.wait_ge(gate_ready, UNITS * T + j + 1)
                if j >= 2:
                    act.wait_ge(weighted_done, PAIRS * T + j - 1)
                elif j == 1:
                    wait(act, h_done, UNITS * T)
                else:
                    wait(act, weighted_done, PAIRS * T)
                nc.scalar.activation(silu[g][0:rows, :], bank[0:rows, G_BANK[g], :], ACT.Silu).then_inc(silu_done, 1)

            def ffn_h_hi(T, q, j):
                rows = P if j < PAIRS else INTER
                act.wait_ge(h_done, UNITS * T + j + 1)
                wait(act, down_done, UNITS * T + j - 2)
                copy(h_h[j % 3][0:rows, :], h[(q + j) % 2][0:rows, :]).then_inc(h_hi_done, 1)

            def ffn_yT(T, q):
                act.wait_ge(down_done, UNITS * (T + 1))
                wait(act, y_ready, T)
                copy(yT, bank[:, Y_BANK[q], :]).then_inc(yT_done, 1)

            def ffn_tile(T, Tx, q, first, last):
                for j in range(UNITS):
                    if j == 0 and not last:
                        ffn_xh(T + 1, 1 - q)
                    if j == 7 and not last:
                        ffn_combT(T + 1, 1 - q)
                    ffn_silu(T, q, j)
                    if j >= 1:
                        ffn_h_hi(T, q, j - 1)
                    elif not first:
                        ffn_h_hi(T - 1, 1 - q, UNITS - 1)
                    if j == 2 and not last:
                        ffn_gsilu(T + 1)
                    if j == LAG and not first:
                        ffn_yT(T - 1, 1 - q)
                    if j == 7 and not last:
                        ffn_xn(T + 2, Tx + 2)

            def ffn(base):
                ffn_phase(base)
                start = base == 0
                if start:
                    act.wait_ge(gate_loaded, 16 * 3)
                    copy(gw_hl[:, 0:NEXP], gw_f[:]).then_inc(gw_hi, 1)
                    act.wait_ge(w13_loaded[0], 16)
                    copy(w13_h[:, early[0], :], w13_f[:, early[0], :]).then_inc(w13_hi[0], 1)
                ffn_xn(base, 0)
                ffn_xh(base, 0)
                if start:
                    act.wait_ge(w13_loaded[1], 16)
                    copy(w13_h[:, early[1], :], w13_f[:, early[1], :]).then_inc(w13_hi[1], 1)
                ffn_gsilu(base)
                ffn_xn(base + 1, 1)
                if start:
                    act.wait_ge(w2_loaded, 16)
                    copy(w2_h[:], w2_f).then_inc(w2_hi, 1)
                ffn_combT(base, 0)
                ffn_tile(base, 0, 0, True, False)
                if start:
                    act.wait_ge(attn_loaded, 16 * 4)
                    copy(wqkv_h[:], wqkv_f).then_inc(wqkv_hi, 1)
                    copy(mask[:], mask_f).then_inc(consts_rounded, 1)
                    copy(ident_r[:], ident[:]).then_inc(consts_rounded, 1)
                with act.Fori(0, TILES // 2 - 1) as k:
                    ffn_tile(base + 2 * k + 1, 2 * k + 1, 1, False, False)
                    ffn_tile(base + 2 * k + 2, 2 * k + 2, 0, False, False)
                T = base + TILES - 1
                ffn_tile(T, TILES - 1, 1, False, True)
                ffn_h_hi(T, 1, UNITS - 1)
                ffn_yT(T, 1)

            def attn_item(item, b, p):
                kind, n = item
                m = M_BANK[ITEMS.index(item) % 2]
                if kind == "xnT":
                    act.wait_ge(a_xnT_ready, 2 * b + n + 1)
                    copy(xh[n][:], bank[:, m, :]).then_inc(a_xh_done, 1)
                elif kind == "qkv":
                    act.wait_ge(qkv_ready, QB * b + n + 1)
                    copy(qkv[p][:, n, :], bank[:, m, 0:3 * D]).then_inc(qkv_done, 1)
                else:
                    act.wait_ge(qkT_ready, QB // 2 * b + n + 1)
                    copy(qkT_h[p][:, :, 2 * P * n:2 * P * (n + 1)],
                         bank[:, m, :].rearrange("p (w c) -> p w c", w=2)).then_inc(qkT_h_done, 1)

            def attn_exp(b, p, i):
                s, w = i % 2, (i + 1) * P
                act.wait_ge(negmax_done, QB * b + i + 1)
                if i >= 2:
                    act.wait_ge(probT_ready, PT_CHUNKS * b + chunk_index(i - 2, 1) + 1)
                else:
                    wait(act, probT_ready, PT_CHUNKS * (b - 1) + chunk_index(QB - 2 + i, 1) + 1)
                nc.scalar.activation(prob[s][:, 0:w],
                                     bank[:, 2 * s:2 * s + 2, :].rearrange("p a c -> p (a c)")[:, 0:w],
                                     ACT.Exp, bias=negmax[s][:],
                                     accum_out=rowsum[p][:, i:i + 1]).then_inc(exp_done, 1)

            def attn_probT(b, i, c):
                s, m = i % 2, chunk_index(i, c)
                blocks = min(4, i + 1 - 4 * c)
                act.wait_ge(probT_ready, PT_CHUNKS * b + m + 1)
                if c == 0 and i >= 2:
                    act.wait_ge(pv_ready, QB * b + i - 1)
                elif c == 0:
                    wait(act, pv_ready, QB * (b - 1) + QB - 1 + i)
                copy(probT[s][:, 4 * c:4 * c + blocks, :].rearrange("p a c -> p (a c)"),
                     bank[:, PT_BANK, 0:blocks * P]).then_inc(probT_done, 1)

            def attn_batch(b, p, last):
                for i in range(QB):
                    items = [] if last else STEP_ITEMS[i]
                    attn_probT(b, i, 0)
                    for item in items[:1]:
                        attn_item(item, b + 1, 1 - p)
                    if i >= 4:
                        attn_probT(b, i, 1)
                    if i + 1 < QB:
                        attn_exp(b, p, i + 1)
                    elif not last:
                        attn_exp(b + 1, 1 - p, 0)
                    for item in items[1:]:
                        attn_item(item, b + 1, 1 - p)

            ffn(0)
            for item in ITEMS:
                attn_item(item, 0, 0)
            attn_exp(0, 0, 0)
            attn_batch(0, 0, False)
            with act.Fori(0, B // 2 - 1) as k:
                attn_batch(2 * k + 1, 1, False)
                attn_batch(2 * k + 2, 0, False)
            attn_batch(B - 1, 1, True)
            ffn(TILES)

        @block.vector
        def _(dve):
            def low_half(lo, f, hi, done):
                nc.vector.tensor_tensor(lo, f, hi.bitcast(F32), ALU.subtract).then_inc(done, 1)

            def ln_stats(blocks, first_block, done, at=0):
                for n in range(blocks):
                    ins = nc.vector.bn_stats(stats[:, at + n, :], X[:, bass.ds(first_block + n, 1), :].rearrange("p a d -> p (a d)"))
                ins.then_inc(done, 1)

            def ln_mean_var(blocks, count, mv_sem, var_sem):
                for n in range(blocks):
                    ins = nc.vector.bn_aggr(mv[:, n, :], stats[:, n, :])
                ins.then_inc(mv_sem, 1)
                dve.wait_ge(mv_sem, count)
                nc.vector.tensor_scalar_add(var_eps[:, 0:blocks], mv[:, 0:blocks, 1], EPS).then_inc(var_sem, 1)

            def ln_apply(blocks, first_block, done, at=0):
                for n in range(at, at + blocks):
                    ins = nc.vector.tensor_scalar(xn[:, n, :], X[:, bass.ds(first_block + n - at, 1), :].rearrange("p a d -> p (a d)"),
                                                  mv[:, n, 0:1], rstd[:, n:n + 1], ALU.subtract, ALU.mult)
                ins.then_inc(done, 1)

            def ffn_xl(T, q):
                dve.wait_ge(xh_done, T + 1)
                nc.vector.tensor_tensor(xl[q][:], bank[:, T_BANK, :], xh[q][:].bitcast(F32),
                                        ALU.subtract).then_inc(xl_done, 1)

            def ffn_logit0(T):
                dve.wait_ge(logits_ready, T + 1)
                nc.vector.reduce_sum(logit0[:], bank[:, T_BANK, 0:NB * 2 * NEXP].rearrange("p (n a e) -> p n e a", n=NB, a=2),
                                     AX_X).then_inc(route_step, 1)

            def ffn_clamp(T):
                dve.wait_ge(route_step, ROUTE * T + 1)
                nc.vector.tensor_scalar(near0[:], logit0[:], -TINY, TINY, ALU.max, ALU.min).then_inc(route_step, 1)

            def ffn_near0(T):
                dve.wait_ge(route_step, ROUTE * T + 2)
                nc.vector.tensor_tensor(near0[:], near0[:], logit0[:], ALU.is_equal).then_inc(route_step, 1)

            def ffn_logit(T):
                dve.wait_ge(route_step, ROUTE * T + 3)
                nc.vector.scalar_tensor_tensor(logit[:], near0[:], 2 * TINY, logit0[:], ALU.mult, ALU.add).then_inc(route_step, 1)

            def ffn_recip(T):
                dve.wait_ge(route_step, ROUTE * T + 4)
                nc.vector.reciprocal(rlogit[:], logit[:]).then_inc(route_step, 1)

            def ffn_score(T):
                dve.wait_ge(gsilu_done, T + 1)
                dve.wait_ge(route_step, ROUTE * T + 5)
                nc.vector.tensor_tensor(score[:], gsilu[:], rlogit[:], ALU.mult).then_inc(route_step, 1)

            def ffn_bias(T):
                dve.wait_ge(route_step, ROUTE * T + 6)
                nc.vector.tensor_tensor(biased[:, :, 0:NEXP], score[:],
                                        gb[:].rearrange("p (a e) -> p a e", a=1).to_broadcast([P, NB, NEXP]),
                                        ALU.add).then_inc(route_step, 1)

            def ffn_biased(T):
                dve.wait_ge(route_step, ROUTE * T + 7)

            def ffn_max(T):
                for n in range(NB):
                    ins = nc.vector.max(top8[:, n, :], biased[:, n, 0:NEXP])
                ins.then_inc(route_step, 1)

            def ffn_top(T):
                dve.wait_ge(route_step, ROUTE * T + 8)
                nc.vector.tensor_copy(take[:, :, 0:TOPK], top8[:, :, 0:TOPK]).then_inc(route_step, 1)

            def ffn_take(T):
                dve.wait_ge(route_step, ROUTE * T + 9)

            def ffn_mark(T):
                for n in range(NB):
                    ins = nc.vector.match_replace(marked[:, n, :], take[:, n, :], biased[:, n, :], TAKEN)
                ins.then_inc(route_step, 1)

            def ffn_chosen(T):
                dve.wait_ge(route_step, ROUTE * T + 10)
                nc.vector.tensor_tensor(chosen[:], marked[:, :, 0:NEXP], biased[:, :, 0:NEXP],
                                        ALU.not_equal).then_inc(route_step, 1)

            def ffn_wsel(T):
                dve.wait_ge(route_step, ROUTE * T + 11)
                nc.vector.tensor_tensor(wsel[:], score[:], chosen[:], ALU.mult).then_inc(route_step, 1)

            def ffn_wsum(T):
                dve.wait_ge(route_step, ROUTE * T + 12)
                nc.vector.reduce_sum(wsum[:], wsel[:], AX_X).then_inc(route_step, 1)

            def ffn_rsum(T):
                dve.wait_ge(route_step, ROUTE * T + 13)
                nc.vector.reciprocal(rsum[:], wsum[:]).then_inc(route_step, 1)

            def ffn_comb(T):
                dve.wait_ge(route_step, ROUTE * T + 14)
                wait(dve, combT_ready, T)
                nc.vector.scalar_tensor_tensor(comb[:], wsel[:], ROUTE_SCALE,
                                               rsum[:].rearrange("p (n e) -> p n e", e=1).to_broadcast([P, NB, NEXP]),
                                               ALU.mult, ALU.mult).then_inc(route_step, 1)

            def ffn_weighted(T, q, j):
                dve.wait_ge(silu_done, UNITS * T + j + 1)
                dve.wait_ge(comb_loaded[j * COMB_LOADS // PAIRS], 32 * (T + 1))
                nc.vector.tensor_tensor(weighted[j % 2], silu[(q + j) % 2], comb_b[q][:, j, :], ALU.mult).then_inc(weighted_done, 1)

            def ffn_h(T, q, j):
                g = (q + j) % 2
                wait(dve, h_lo_done, UNITS * T + j - 1)
                if j < PAIRS:
                    dve.wait_ge(weighted_done, PAIRS * T + j + 1)
                    dve.wait_ge(up_ready, PAIRS * T + j + 1)
                    nc.vector.tensor_tensor(h[g], weighted[j % 2], bank[:, U_BANK[j % 2], :], ALU.mult).then_inc(h_done, 1)
                else:
                    dve.wait_ge(silu_done, UNITS * T + j + 1)
                    nc.vector.tensor_tensor(h[g][0:INTER, :], silu[g][0:INTER, :], bank[INTER:P, G_BANK[g], :],
                                            ALU.mult).then_inc(h_done, 1)

            def ffn_stats(T, Tx, n):
                ins = nc.vector.bn_stats(stats[:, n, :], X[:, bass.ds(NB * Tx + n, 1), :].rearrange("p a d -> p (a d)"))
                if n == NB - 1:
                    ins.then_inc(stats_done, 1)

            def ffn_stats_wait(T):
                dve.wait_ge(stats_done, ln_count(T))

            def ffn_mv(T):
                for n in range(NB):
                    ins = nc.vector.bn_aggr(mv[:, n, :], stats[:, n, :])
                ins.then_inc(mv_done, 1)

            def ffn_var(T):
                dve.wait_ge(mv_done, ln_count(T))
                nc.vector.tensor_scalar_add(var_eps[:, 0:NB], mv[:, 0:NB, 1], EPS).then_inc(var_done, 1)

            def residual(T, Tx):
                dve.wait_ge(y_ready, T + 1)
                xt = X[:, tile_blocks(Tx), :]
                nc.vector.scalar_tensor_tensor(xt, bank[:, YT_BANK, :].rearrange("p (n d) -> p n d", n=NB), 0.5, xt,
                                               ALU.mult, ALU.add).then_inc(x_done, 1)

            def ffn_tile(T, Tx, q, first, last):
                N, L, Lx = T + 1, T + 2, Tx + 2
                if last:
                    for j in range(PAIRS):
                        ffn_weighted(T, q, j)
                        if j == 7 and not first:
                            residual(T - 1, Tx - 1)
                        ffn_h(T, q, j)
                    ffn_h(T, q, PAIRS)
                    return
                ffn_xl(N, 1 - q)
                ffn_weighted(T, q, 0)
                ffn_stats(L, Lx, 0)
                ffn_h(T, q, 0)
                ffn_logit0(N)
                ffn_weighted(T, q, 1)
                ffn_clamp(N)
                ffn_h(T, q, 1)
                ffn_near0(N)
                ffn_stats(L, Lx, 1)
                ffn_logit(N)
                ffn_weighted(T, q, 2)
                ffn_recip(N)
                ffn_h(T, q, 2)
                ffn_score(N)
                ffn_stats(L, Lx, 2)
                ffn_bias(N)
                ffn_biased(N)
                ffn_weighted(T, q, 3)
                ffn_max(N)
                ffn_h(T, q, 3)
                ffn_top(N)
                ffn_take(N)
                ffn_weighted(T, q, 4)
                ffn_mark(N)
                ffn_h(T, q, 4)
                ffn_chosen(N)
                ffn_stats(L, Lx, 3)
                ffn_wsel(N)
                ffn_weighted(T, q, 5)
                ffn_wsum(N)
                ffn_stats_wait(L)
                ffn_h(T, q, 5)
                ffn_rsum(N)
                ffn_mv(L)
                ffn_comb(N)
                ffn_weighted(T, q, 6)
                ffn_var(L)
                ffn_h(T, q, 6)
                ffn_weighted(T, q, 7)
                if not first:
                    residual(T - 1, Tx - 1)
                ffn_h(T, q, 7)
                ffn_h(T, q, 8)

            def ffn(base):
                ffn_phase(base)
                start = base == 0
                if start:
                    dve.wait_ge(x_loaded[0], 16)
                for n in range(NB):
                    ffn_stats(base, 0, n)
                ffn_stats_wait(base)
                ffn_mv(base)
                ffn_var(base)
                if start:
                    dve.wait_ge(gw_hi, 1)
                    low_half(gw_hl[:, NEXP:2 * NEXP], gw_f[:], gw_hl[:, 0:NEXP], gw_split)
                    dve.wait_ge(w13_hi[0], 1)
                    low_half(w13_l[:, early[0], :], w13_f[:, early[0], :], w13_h[:, early[0], :], w13_split[0])
                ffn_xl(base, 0)
                if start:
                    dve.wait_ge(x_loaded[1], 16)
                for n in range(NB):
                    ffn_stats(base + 1, 1, n)
                ffn_logit0(base)
                ffn_clamp(base)
                ffn_stats_wait(base + 1)
                ffn_near0(base)
                ffn_mv(base + 1)
                ffn_logit(base)
                ffn_var(base + 1)
                ffn_recip(base)
                if start:
                    dve.wait_ge(consts_set, 5)
                ffn_score(base)
                ffn_bias(base)
                ffn_biased(base)
                ffn_max(base)
                ffn_top(base)
                ffn_take(base)
                ffn_mark(base)
                ffn_chosen(base)
                ffn_wsel(base)
                ffn_wsum(base)
                ffn_rsum(base)
                ffn_comb(base)
                ffn_tile(base, 0, 0, True, False)
                if start:
                    dve.wait_ge(x_loaded[2], 16)
                with dve.Fori(0, TILES // 2 - 1) as k:
                    ffn_tile(base + 2 * k + 1, 2 * k + 1, 1, False, False)
                    ffn_tile(base + 2 * k + 2, 2 * k + 2, 0, False, False)
                ffn_tile(base + TILES - 1, TILES - 1, 1, False, True)
                residual(base + TILES - 1, TILES - 1)

            def attn_item(item, b, p):
                kind, n = item
                m = M_BANK[ITEMS.index(item) % 2]
                if kind == "xnT":
                    dve.wait_ge(a_xh_done, 2 * b + n + 1)
                    nc.vector.tensor_tensor(xl[n][:], bank[:, m, :], xh[n][:].bitcast(F32),
                                            ALU.subtract).then_inc(a_xl_done, 1)
                elif kind == "qkv":
                    s = n % ROPE_BUFS
                    dve.wait_ge(qkv_done, QB * b + n + 1)
                    wait(dve, rot_done, QB * b + n - ROPE_BUFS + 1)
                    nc.vector.tensor_tensor(rope_c[s][:], qkv[p][:, n, 0:2 * D].rearrange("p (w d) -> p w d", w=2),
                                            cos[:, n, :, :], ALU.mult).then_inc(rope_c_done, 1)
                else:
                    dve.wait_ge(qkT_h_done, QB // 2 * b + n + 1)
                    cols = slice(2 * P * n, 2 * P * (n + 1))
                    nc.vector.tensor_tensor(qkT_l[p][:, :, cols], bank[:, m, :].rearrange("p (w c) -> p w c", w=2),
                                            qkT_h[p][:, :, cols].bitcast(F32), ALU.subtract).then_inc(qkT_l_done, 1)

            def attn_max(b, i):
                s, w = i % 2, (i + 1) * P
                wait(dve, exp_done, QB * b + i - 1)
                dve.wait_ge(scores_ready, QB * b + i + 1)
                nc.vector.reduce_max(negmax[s][:], bank[:, 2 * s:2 * s + 2, :].rearrange("p a c -> p (a c)")[:, 0:w],
                                     AX_X, negate=True).then_inc(negmax_done, 1)

            def attn_rrow(b, p, i):
                dve.wait_ge(exp_done, QB * b + i + 1)
                nc.vector.reciprocal(rrow[p][:, i:i + 1], rowsum[p][:, i:i + 1]).then_inc(rrow_done, 1)

            def attn_residual(b, p, i):
                dve.wait_ge(rrow_done, QB * b + i + 1)
                dve.wait_ge(pv_ready, QB * b + i + 1)
                xb = X[:, bass.ds(QB * b + i, 1), :].rearrange("p a d -> p (a d)")
                nc.vector.scalar_tensor_tensor(xb, bank[:, O_BANK, 0:D], rrow[p][:, i:i + 1], xb,
                                               ALU.mult, ALU.add).then_inc(attn_done, 1)

            def attn_stats(b):
                dve.wait_ge(a_stats_done, 2 * b + 2)

            def attn_ln(b, part):
                if part < 2:
                    ln_stats(NB, QB * b + NB * part, a_stats_done, NB * part)
                elif part == 2:
                    ln_mean_var(QB, b + 1, a_mv_done, a_var_done)
                else:
                    half = part - 3
                    dve.wait_ge(a_rstd_done, b + 1)
                    wait(dve, a_xnT_ready, 2 * (b - 1) + half + 1)
                    ln_apply(NB, QB * b + NB * half, a_xn_done, NB * half)

            def attn_batch(b, p, first, last):
                for i in range(QB):
                    if i >= 1:
                        attn_residual(b, p, i - 1)
                    elif not first:
                        attn_residual(b - 1, 1 - p, QB - 1)
                    if i == 5 and not last:
                        attn_stats(b + 2)
                    if i + 1 < QB:
                        attn_max(b, i + 1)
                    elif not last:
                        attn_max(b + 1, 0)
                    attn_rrow(b, p, i)
                    if not last:
                        for item in STEP_ITEMS[i]:
                            attn_item(item, b + 1, 1 - p)
                        if i >= 3:
                            attn_ln(b + 2, i - 3)

            ffn(0)
            dve.wait_ge(attn_loaded, 16 * 4)
            dve.wait_ge(x_done, TILES)
            def attn_row_ln(b):
                for part in range(5):
                    if part == 2:
                        attn_stats(b)
                    attn_ln(b, part)

            attn_row_ln(0)
            for item in ITEMS:
                attn_item(item, 0, 0)
            attn_row_ln(1)
            attn_max(0, 0)
            attn_batch(0, 0, True, False)
            with dve.Fori(0, B // 2 - 1) as k:
                attn_batch(2 * k + 1, 1, False, False)
                attn_batch(2 * k + 2, 0, False, False)
            attn_batch(B - 1, 1, False, True)
            attn_residual(B - 1, 1, QB - 1)
            dve.wait_ge(attn_done, B * QB)
            ffn(TILES)

        @block.tensor
        def _(pe):
            def mm(dst, lhsT, rhs, start, stop):
                return nc.tensor.matmul(dst, lhsT, rhs, start=start, stop=stop)

            def mm3(dst, lh, ll, rh, rl, start=True, stop=True):
                mm(dst, lh, rh, start, False)
                mm(dst, lh, rl, False, False)
                return mm(dst, ll, rh, False, stop)

            def ffn_xnT(T):
                pe.wait_ge(xn_done, ln_count(T))
                wait(pe, combT_done, T)
                for n in range(NB):
                    ins = nc.tensor.transpose(bank[:, T_BANK, n * P:(n + 1) * P], xn[:, n, :], ident[:])
                ins.then_inc(xnT_ready, 1)

            def ffn_logits(T, q):
                pe.wait_ge(xl_done, T + 1)
                for n in range(NB):
                    blk, at = slice(n * P, (n + 1) * P), 2 * NEXP * n
                    mm(bank[:, T_BANK, at:at + 2 * NEXP], xh[q][:, blk], gw_hl[:], True, False)
                    ins = mm(bank[:, T_BANK, at:at + NEXP], xl[q][:, blk], gw_hl[:, 0:NEXP], False, True)
                ins.then_inc(logits_ready, 1)

            def ffn_combT(T):
                pe.wait_ge(route_step, ROUTE * (T + 1))
                for n in range(NB):
                    ins = nc.tensor.transpose(bank[0:NEXP, T_BANK, n * P:(n + 1) * P], comb[:, n, :], ident[:])
                ins.then_inc(combT_ready, 1)

            def ffn_y(T):
                pe.wait_ge(yT_done, T + 1)
                wait(pe, x_done, T)
                for n in range(NB):
                    ins = nc.tensor.transpose(bank[:, YT_BANK, n * P:(n + 1) * P], yT[:, n * P:(n + 1) * P], ident[:])
                ins.then_inc(y_ready, 1)

            def ffn_up(T, q, j):
                g, c = (q + j) % 2, j % 2
                if j == 1:
                    wait(pe, h_done, UNITS * T)
                else:
                    wait(pe, silu_done, UNITS * T + j - 1)
                mm3(bank[:, G_BANK[g], :], w13_h[:, 2 * j, :], w13_l[:, 2 * j, :], xh[q][:], xl[q][:]).then_inc(gate_ready, 1)
                if j < PAIRS:
                    if j >= 2:
                        pe.wait_ge(h_done, UNITS * T + j - 1)
                    else:
                        wait(pe, h_done, UNITS * (T - 1) + PAIRS - 1 + j)
                    mm3(bank[:, U_BANK[c], :], w13_h[:, 2 * j + 1, :], w13_l[:, 2 * j + 1, :],
                        xh[q][:], xl[q][:]).then_inc(up_ready, 1)

            def ffn_down(T, q, j):
                pe.wait_ge(h_lo_done, UNITS * T + j + 1)
                if j == 0:
                    wait(pe, yT_done, T - 1)
                Y, k = bank[:, Y_BANK[q], :], j % 3
                if j < PAIRS:
                    mm(Y, w2_h[:, j, :], h_h[k][:], j == 0, False)
                    mm(Y, w2_l[:, j, :], h_h[k][:], False, False)
                    ins = mm(Y, w2_h[:, j, :], h_l[k][:], False, False)
                else:
                    mm(Y, w2_h[:, j, :], h_h[k][:], False, False)
                    ins = mm(Y, w2_l[:, j, :], h_h[k][:], False, True)
                ins.then_inc(down_done, 1)

            def ffn_tile(T, q, first, last, start):
                if not first and not last:
                    ffn_xnT(T + 1)
                for j in range(UNITS):
                    if start and j == EARLY:
                        pe.wait_ge(w13_split[1], 1)
                        pe.wait_ge(w2_split, 1)
                    ffn_up(T, q, j)
                    if first and j == 0:
                        ffn_combT(T)
                        ffn_xnT(T + 1)
                    if j >= LAG:
                        ffn_down(T, q, j - LAG)
                    elif not first:
                        ffn_down(T - 1, 1 - q, UNITS - LAG + j)
                    if j == (1 if first else 0) and not last:
                        ffn_logits(T + 1, 1 - q)
                    if j == 4 and not first:
                        ffn_y(T - 1)
                    if j == 6 and not last:
                        ffn_combT(T + 1)

            def ffn(base):
                ffn_phase(base)
                start = base == 0
                if start:
                    pe.wait_ge(gate_loaded, 16 * 3)
                ffn_xnT(base)
                if start:
                    pe.wait_ge(gw_split, 1)
                ffn_logits(base, 0)
                if start:
                    pe.wait_ge(w13_split[0], 1)
                ffn_tile(base, 0, True, False, start)
                with pe.Fori(0, TILES // 2 - 1) as k:
                    ffn_tile(base + 2 * k + 1, 1, False, False, False)
                    ffn_tile(base + 2 * k + 2, 0, False, False, False)
                T = base + TILES - 1
                ffn_tile(T, 1, False, True, False)
                for j in range(UNITS - LAG, UNITS):
                    ffn_down(T, 1, j)
                ffn_y(T)

            def attn_item(item, b, p):
                kind, n = item
                at = ITEMS.index(item)
                m = M_BANK[at % 2]
                kind2, n2 = ITEMS[at - 2]
                if at < 2:
                    wait(pe, qkT_l_done, QB // 2 * (b - 1) + n2 + 1)
                elif kind2 == "xnT":
                    pe.wait_ge(a_xl_done, 2 * b + n2 + 1)
                elif kind2 == "qkv":
                    pe.wait_ge(qkv_done, QB * b + n2 + 1)
                else:
                    pe.wait_ge(qkT_l_done, QB // 2 * b + n2 + 1)
                if kind == "xnT":
                    pe.wait_ge(a_xn_done, 2 * b + n + 1)
                    for a in range(NB):
                        ins = nc.tensor.transpose(bank[:, m, a * P:(a + 1) * P], xn[:, NB * n + a, :], ident[:])
                    ins.then_inc(a_xnT_ready, 1)
                elif kind == "qkv":
                    a, blk = n // NB, slice(n % NB * P, (n % NB + 1) * P)
                    pe.wait_ge(a_xl_done, 2 * b + a + 1)
                    mm3(bank[:, m, 0:3 * D], xh[a][:, blk], xl[a][:, blk], wqkv_h[:], wqkv_l[:]).then_inc(qkv_ready, 1)
                else:
                    pe.wait_ge(rot_done, QB * b + 2 * n + 2)
                    for a in range(2):
                        for w in range(2):
                            c = w * 2 * P + a * P
                            ins = nc.tensor.transpose(bank[:, m, c:c + P], rot[(2 * n + a) % ROPE_BUFS][:, w, :], ident[:])
                    ins.then_inc(qkT_ready, 1)

            def attn_scores(b, p, i):
                s = i % 2
                pe.wait_ge(qkT_l_done, QB // 2 * b + i // 2 + 1)
                wait(pe, exp_done, QB * b + i - 1)
                qs = slice(i * P, (i + 1) * P)
                for c in range(1 + i // 4):
                    k0, k1 = 512 * c, min(512 * (c + 1), (i + 1) * P)
                    dst = bank[:, 2 * s + c, 0:k1 - k0]
                    diag = c == i // 4
                    ins = mm3(dst, qkT_h[p][:, 0, qs], qkT_l[p][:, 0, qs], qkT_h[p][:, 1, k0:k1], qkT_l[p][:, 1, k0:k1],
                              True, not diag)
                    if diag:
                        ins = mm(bank[:, 2 * s + c, k1 - k0 - P:k1 - k0], ident_r[:], mask[:], False, True)
                ins.then_inc(scores_ready, 1)

            def attn_probT(b, i, c):
                s, m = i % 2, chunk_index(i, c)
                if c == 0:
                    pe.wait_ge(exp_done, QB * b + i + 1)
                wait(pe, probT_done, PT_CHUNKS * b + m)
                blocks = min(4, i + 1 - 4 * c)
                for a in range(blocks):
                    k0 = (4 * c + a) * P
                    ins = nc.tensor.transpose(bank[:, PT_BANK, a * P:(a + 1) * P], prob[s][:, k0:k0 + P], ident[:])
                ins.then_inc(probT_ready, 1)

            def attn_pv(b, p, i):
                s = i % 2
                wait(pe, attn_done, QB * b + i)
                for kb in range(i + 1):
                    if kb % 4 == 0:
                        pe.wait_ge(probT_done, PT_CHUNKS * b + chunk_index(i, kb // 4) + 1)
                    ins = mm(bank[:, O_BANK, 0:D], probT[s][:, kb, :], qkv[p][:, kb, 2 * D:3 * D], kb == 0, kb == i)
                ins.then_inc(pv_ready, 1)

            def attn_batch(b, p, last):
                for i in range(QB):
                    if i + 1 < QB:
                        attn_scores(b, p, i + 1)
                    elif not last:
                        attn_scores(b + 1, 1 - p, 0)
                    items = [] if last else STEP_ITEMS[i]
                    attn_probT(b, i, 0)
                    for item in items[:1]:
                        attn_item(item, b + 1, 1 - p)
                    if i >= 4:
                        attn_probT(b, i, 1)
                    for item in items[1:]:
                        attn_item(item, b + 1, 1 - p)
                    attn_pv(b, p, i)

            ffn(0)
            pe.wait_ge(wqkv_split, 1)
            pe.wait_ge(consts_rounded, 2)
            pe.wait_ge(x_done, TILES)
            for item in ITEMS:
                attn_item(item, 0, 0)
            attn_scores(0, 0, 0)
            attn_batch(0, 0, False)
            with pe.Fori(0, B // 2 - 1) as k:
                attn_batch(2 * k + 1, 1, False)
                attn_batch(2 * k + 2, 0, False)
            attn_batch(B - 1, 1, True)
            pe.wait_ge(attn_done, B * QB)
            ffn(TILES)


def chunk_index(i, c):
    c = min(c, i // 4)
    return i if i < 4 else 4 + 2 * (i - 4) + c


def rope_tables():
    f = np.float32
    i = np.arange(D // 2, dtype=f)
    theta = np.power(f(10000.0), (f(-2.0) * (i - f(1.0)) / f(D)).astype(f)).astype(f)
    ang = (np.arange(M, dtype=f)[:, None] * theta[None, :]).astype(f).astype(np.float64)
    c = np.repeat(np.cos(ang).astype(f), 2, axis=1)
    s = np.repeat(np.sin(ang).astype(f), 2, axis=1)
    s[:, 1::2] *= -1
    scale = np.array([SCORE_SCALE, 1.0])[:, None]
    return [(t.reshape(QB, P, 1, D).astype(np.float64) * scale).astype(f).transpose(1, 0, 2, 3) for t in (c, s)]


def kernel(**inputs):
    import concourse.bacc as bacc
    from concourse.bass_utils import run_bass_kernel_spmd

    a = {k: np.asarray(v) for k, v in inputs.items()}
    w13 = a["L0_ffn_w13"].reshape(PAIRS, 2, 2, INTER, D).transpose(4, 0, 2, 1, 3).reshape(D, 2 * PAIRS, P)
    w13T = np.concatenate([w13, a["L0_ffn_w13_s"].T.reshape(D, 1, P)], axis=1)
    w2 = a["L0_ffn_w2"].reshape(PAIRS, 2, D, INTER).transpose(1, 3, 0, 2).reshape(P, PAIRS, D)
    w2s = np.concatenate([a["L0_ffn_w2_s"].T, a["L0_ffn_w2_s"].T], axis=0)
    w2T = np.concatenate([w2, w2s.reshape(P, 1, D)], axis=1)
    wqkvT = np.concatenate([a["L0_attn_w_q"].T, a["L0_attn_w_k"].T, a["L0_attn_w_v"].T], axis=1)
    row, col = np.arange(P)[:, None], np.arange(P)[None, :]
    mask = np.where(col > row, np.float32(MASKED), np.float32(0.0)).astype(np.float32)
    cos, sin = rope_tables()
    arrays = {
        "x": a["L0_attn_x"], "w13T": w13T, "w2T": w2T, "wqkvT": wqkvT, "gwT": a["L0_ffn_gate_w"].T,
        "gate_b": np.tile(a["L0_ffn_gate_b"].reshape(1, NEXP), (P, 1)),
        "ident": np.eye(P, dtype=np.float32), "mask": mask, "cos": cos, "sin": sin,
    }
    arrays = {f"in_{k}": np.ascontiguousarray(v) for k, v in arrays.items()}
    nc = bacc.Bacc("TRN2", target_bir_lowering=False, num_devices=1)
    args = [nc.dram_tensor(k, v.shape, mybir.dt.from_np(v.dtype), kind="ExternalInput").ap() for k, v in arrays.items()]
    args.append(nc.dram_tensor("comb_rows", (2, NEXP, TILE), F32, kind="Internal").ap())
    args.append(nc.dram_tensor("out_x", (B, M, D), F32, kind="ExternalOutput").ap())
    macaron(nc, *args)
    r = run_bass_kernel_spmd(nc, [arrays], core_ids=[0])
    return r.results[0]["out_x"]
```

```python
from contextlib import ExitStack

import numpy as np

import concourse.bass as bass
from concourse import mybir

P = 128
B, M, D = 8, 1024, 128
INTER, NEXP, TOPK = 64, 16, 4
ROUTE_SCALE = 2.5
EPS = 1e-5
TILE = 512
NB = TILE // P
TILES = B * M // TILE
PAIRS = NEXP * INTER // P
UNITS = PAIRS + 1
QB = M // P
SCORE_SCALE = float(1.0 / np.sqrt(np.float32(D)))
MASKED = -3.0e38
SENTINEL, TAKEN = -3.0e38, 3.0e38
TINY = 1.0e-30
ROUTE = 15
PT_CHUNKS = 12

F32 = mybir.dt.float32
F32R = mybir.dt.float32r
ALU = mybir.AluOpType
ACT = mybir.ActivationFunctionType
AX_X = mybir.AxisListType.X

G_BANK, U_BANK, YT_BANK, Y_BANK, T_BANK = (0, 1), (2, 3), 4, (5, 6), 7
PT_BANK, O_BANK, M_BANK = 4, 6, (5, 7)

STEP_ITEMS = [[("xnT", 0), ("xnT", 1)], [("qkv", 0), ("qkv", 1), ("qkv", 2)], [("qkv", 3), ("qkv", 4), ("qkT", 0)],
              [("qkv", 5), ("qkT", 1)], [("qkv", 6), ("qkv", 7), ("probT", 4)],
              [("qkT", 2), ("probT", 5)], [("qkT", 3), ("probT", 6)], [("probT", 7)]]
SLOTS = [item for step in STEP_ITEMS for item in step]
ITEMS = [item for item in SLOTS if item[0] != "probT"]


TAIL_UNIT = 5
TAIL_ITEMS = ITEMS[:UNITS - TAIL_UNIT]
NEXT_ITEMS = ITEMS[UNITS - TAIL_UNIT:]


def m_bank(item, prologue=False):
    return M_BANK[(ITEMS if prologue else SLOTS).index(item) % 2]


def step_items(step):
    items = STEP_ITEMS[step]
    at = items.index(("probT", step)) if step >= NB else 1
    return items[:at], [item for item in items[at:] if item[0] != "probT"]


ROPE_BUFS = 4
LAG = 3
EARLY = 2
COMB_LOADS = 4


def macaron(nc, x, w13T, w2T, wqkvT, gwT, gate_b, ident_d, mask_d, cos_d, sin_d, comb_d, out):
    x_v = x.rearrange("b (n p) d -> p (b n) d", p=P)
    out_v = out.rearrange("b (n p) d -> p (b n) d", p=P)

    with ExitStack() as ctx:
        def sb(name, shape, dt=F32):
            return ctx.enter_context(nc.sbuf_tensor(name, shape, dt))

        def sem(name):
            return ctx.enter_context(nc.semaphore(name))

        bank = ctx.enter_context(nc.psum_tensor("bank", [P, 8, 512], F32))

        X = sb("X", [P, (B + 1) * QB, D])
        ident = sb("ident", [P, P])
        w13_h = sb("w13_h", [P, UNITS * 2 - 1, P], F32R)
        w13_l = sb("w13_l", [P, UNITS * 2 - 1, P], F32R)
        w2_h = sb("w2_h", [P, UNITS, D], F32R)
        w2_l = sb("w2_l", [P, UNITS, D], F32R)
        wqkv_h = sb("wqkv_h", [P, 3 * D], F32R)
        wqkv_l = sb("wqkv_l", [P, 3 * D], F32R)
        gw_f = sb("gw_f", [P, NEXP])
        gw_hl = sb("gw_hl", [P, 2 * NEXP], F32R)
        gb = sb("gb", [P, NEXP])
        mask = sb("mask", [P, P], F32R)
        ident_r = sb("ident_r", [P, P], F32R)
        cos = sb("cos", [P, QB, 2, D])
        sin = sb("sin", [P, QB, 2, D])
        neg_half = sb("neg_half", [P, QB])

        stats = sb("stats", [P, QB, 6])
        mv = sb("mv", [P, QB, 2])
        var_eps = sb("var_eps", [P, QB])
        rstd = sb("rstd", [P, QB])
        neg_one = sb("neg_one", [P, NB])
        neg_mean = sb("neg_mean", [P, NB])
        neg_shift = sb("neg_shift", [P, NB])
        xn = sb("xn", [P, QB, D])
        xh = [sb(f"xh{q}", [P, TILE], F32R) for q in range(3)]
        xl = [sb(f"xl{q}", [P, TILE], F32R) for q in range(3)]
        xh_half, xl_half = (xh[0], xh[2]), (xl[0], xl[2])

        logit0 = sb("logit0", [P, NB, NEXP])
        near0 = sb("near0", [P, NB, NEXP])
        logit = sb("logit", [P, NB, NEXP])
        gsilu = sb("gsilu", [P, NB, NEXP])
        rlogit = sb("rlogit", [P, NB, NEXP])
        score = sb("score", [P, NB, NEXP])
        biased = sb("biased", [P, NB, NEXP + TOPK])
        top8 = sb("top8", [P, NB, 8])
        take = sb("take", [P, NB, 8])
        marked = sb("marked", [P, NB, NEXP + TOPK])
        chosen = sb("chosen", [P, NB, NEXP])
        wsel = sb("wsel", [P, NB, NEXP])
        wsum = sb("wsum", [P, NB])
        rsum = sb("rsum", [P, NB])
        comb = sb("comb", [P, P // NB, NB])
        combT = [sb(f"combT{q}", [NEXP * NB, P]) for q in range(2)]

        h_h = [sb(f"h_h{k}", [P, TILE], F32R) for k in range(3)]
        h_l = [sb(f"h_l{k}", [P, TILE], F32R) for k in range(3)]

        qkv_both = sb("qkv_both", [P, 2, QB, 3 * D])
        qkv = [qkv_both[:, p, :, :] for p in range(2)]
        rope_c = [sb(f"rope_c{p}", [P, 2, D]) for p in range(ROPE_BUFS)]
        rope_s = [sb(f"rope_s{p}", [P, 2, D]) for p in range(ROPE_BUFS)]
        rot = [sb(f"rot{p}", [P, 2, D]) for p in range(ROPE_BUFS)]
        qkT = [sb(f"qkT{p}", [P, 2, 2, M], F32R) for p in range(2)]
        qkT_h = [qkT[p][:, 0, :, :] for p in range(2)]
        qkT_l = [qkT[p][:, 1, :, :] for p in range(2)]
        negmax = [sb(f"negmax{p}", [P, 1]) for p in range(2)]
        rowsum = [sb(f"rowsum{p}", [P, QB]) for p in range(2)]
        rrow = [sb(f"rrow{p}", [P, QB]) for p in range(2)]
        prob = [sb(f"prob{p}", [P, M]) for p in range(2)]
        probT = [sb(f"probT{p}", [P, QB, P]) for p in range(2)]

        comb_b = [qkT[q][:].bitcast(F32).rearrange("p a w m -> p (a w m)").rearrange("p (j t) -> p j t", t=TILE)
                  for q in range(2)]
        silu = [prob[q][:, 0:TILE] for q in range(2)]
        weighted = [prob[q][:, TILE:2 * TILE] for q in range(2)]
        h = [probT[q][:, 0:NB, :].rearrange("p a c -> p (a c)") for q in range(2)]
        yT = probT[0][:, NB:2 * NB, :].rearrange("p a c -> p (a c)")

        staged = qkv_both[:].rearrange("p a n d -> p (a n d)").rearrange("p (n c) -> p n c", c=P)
        parts, at = {}, 0
        for name, blocks in (("w13", 2 * UNITS - 1), ("w2", UNITS), ("wqkv", 3), ("mask", 1)):
            parts[name] = staged[:, at:at + blocks, :]
            at += blocks
        w13_f, w2_f = parts["w13"], parts["w2"]
        wqkv_f, mask_f = (parts[n].rearrange("p n c -> p (n c)") for n in ("wqkv", "mask"))

        x_loaded = [sem(f"x_loaded{n}") for n in range(3)]
        gate_loaded = sem("gate_loaded")
        w13_loaded = [sem(f"w13_loaded{n}") for n in range(2)]
        w2_loaded = sem("w2_loaded")
        attn_loaded = sem("attn_loaded")
        consts_set = sem("consts_set")
        gw_hi = sem("gw_hi")
        w13_hi = [sem(f"w13_hi{n}") for n in range(2)]
        w2_hi = sem("w2_hi")
        wqkv_hi = sem("wqkv_hi")
        consts_rounded = sem("consts_rounded")
        gw_split = sem("gw_split")
        w13_split = [sem(f"w13_split{n}") for n in range(2)]
        w2_split = sem("w2_split")
        wqkv_split = sem("wqkv_split")
        stats_done = sem("stats_done")
        mv_done = sem("mv_done")
        var_done = sem("var_done")
        rstd_done = sem("rstd_done")
        neg_mean_done = sem("neg_mean_done")
        neg_shift_done = sem("neg_shift_done")
        xn_done = sem("xn_done")
        xnT_ready = sem("xnT_ready")
        xh_done = sem("xh_done")
        xl_done = sem("xl_done")
        logits_ready = sem("logits_ready")
        gsilu_done = sem("gsilu_done")
        route_step = sem("route_step")
        combT_ready = sem("combT_ready")
        combT_done = sem("combT_done")
        gate_ready = sem("gate_ready")
        comb_written = sem("comb_written")
        comb_loaded = [sem(f"comb_loaded{n}") for n in range(COMB_LOADS)]
        up_ready = sem("up_ready")
        silu_done = sem("silu_done")
        weighted_done = sem("weighted_done")
        h_done = sem("h_done")
        h_hi_done = sem("h_hi_done")
        h_lo_done = sem("h_lo_done")
        down_done = sem("down_done")
        yT_done = sem("yT_done")
        y_ready = sem("y_ready")
        x_done = sem("x_done")
        stored = sem("stored")
        a_stats_done = sem("a_stats_done")
        a_mv_done = sem("a_mv_done")
        a_var_done = sem("a_var_done")
        a_rstd_done = sem("a_rstd_done")
        a_xn_done = sem("a_xn_done")
        a_xnT_ready = sem("a_xnT_ready")
        a_xh_done = sem("a_xh_done")
        a_xl_done = sem("a_xl_done")
        qkv_ready = sem("qkv_ready")
        qkv_done = sem("qkv_done")
        rope_c_done = sem("rope_c_done")
        rope_s_done = sem("rope_s_done")
        rot_done = sem("rot_done")
        qkT_ready = sem("qkT_ready")
        qkT_h_done = sem("qkT_h_done")
        qkT_l_done = sem("qkT_l_done")
        scores_ready = sem("scores_ready")
        negmax_done = sem("negmax_done")
        exp_done = sem("exp_done")
        probT_ready = sem("probT_ready")
        probT_done = sem("probT_done")
        pv_ready = sem("pv_ready")
        rrow_done = sem("rrow_done")
        attn_done = sem("attn_done")

        early = slice(0, 2 * EARLY), slice(2 * EARLY, 2 * UNITS - 1)

        def wait(eng, s, n):
            if not isinstance(n, int) or n > 0:
                eng.wait_ge(s, n)

        def tile_blocks(T):
            return bass.ds(NB * T, NB)

        def ln_count(T):
            return T + 1 + ln_count.phase

        def ffn_phase(base):
            ln_count.phase = base // TILES

        block = ctx.enter_context(nc.Block())

        @block.sync
        def _(sp):
            def load(dst, src, s):
                sp.dma_start(dst, src).then_inc(s, 16)

            load(X[:, 0:NB, :], x_v[:, 0:NB, :], x_loaded[0])
            load(ident[:], ident_d, gate_loaded)
            load(gw_f[:], gwT, gate_loaded)
            load(gb[:], gate_b, gate_loaded)
            load(w13_f[:, early[0], :], w13T[:, early[0], :], w13_loaded[0])
            load(w13_f[:, early[1], :], w13T[:, early[1], :], w13_loaded[1])
            load(X[:, NB:3 * NB, :], x_v[:, NB:3 * NB, :], x_loaded[1])
            load(w2_f, w2T, w2_loaded)
            load(X[:, 3 * NB:B * QB, :], x_v[:, 3 * NB:, :], x_loaded[2])

            def comb_rows(T, q):
                sp.wait_ge(combT_done, T + 1)
                sp.dma_start(comb_d[q].rearrange("e (n t) -> (e n) t", n=NB), combT[q][:]).then_inc(comb_written, 16)
                sp.wait_ge(comb_written, 16 * (T + 1))
                src = comb_d[q].rearrange("(j a) t -> a j t", a=2)
                n = PAIRS // COMB_LOADS
                for g in range(COMB_LOADS):
                    for a in range(2):
                        sp.dma_start(comb_b[q][a * INTER:(a + 1) * INTER, n * g:n * (g + 1), :],
                                     src[a:a + 1, n * g:n * (g + 1), :].to_broadcast([INTER, n, TILE])
                                     ).then_inc(comb_loaded[g], 16)

            def store(t):
                sp.wait_ge(x_done, TILES + 1 + t)
                sp.dma_start(out_v[:, tile_blocks(t), :], X[:, tile_blocks(t), :]).then_inc(stored, 16)

            def ffn(base, stores):
                comb_rows(base, 0)
                if stores:
                    sp.wait_ge(scores_ready, B * QB)
                else:
                    load(wqkv_f, wqkvT, attn_loaded)
                    load(mask_f, mask_d, attn_loaded)
                    load(cos[:], cos_d, attn_loaded)
                    load(sin[:], sin_d, attn_loaded)
                comb_rows(base + 1, 1)
                with sp.Fori(0, TILES // 2 - 1) as k:
                    for q in range(2):
                        comb_rows(base + 2 * k + 2 + q, q)
                        if stores:
                            store(2 * k + q)
                if stores:
                    store(TILES - 2)
                    store(TILES - 1)

            ffn(0, False)
            sp.wait_ge(scores_ready, (B - 1) * QB)
            ffn(TILES, True)
            sp.wait_ge(stored, 16 * TILES)

        @block.gpsimd
        def _(pool):
            nc.gpsimd.memset(neg_half[:], -0.5).then_inc(consts_set, 1)
            nc.gpsimd.memset(neg_one[:], -1.0).then_inc(consts_set, 1)
            nc.gpsimd.memset(take[:], SENTINEL).then_inc(consts_set, 1)
            nc.gpsimd.memset(biased[:], SENTINEL).then_inc(consts_set, 1)
            nc.gpsimd.memset(comb[:], 0.0).then_inc(consts_set, 1)
            nc.gpsimd.memset(X[:, B * QB:, :], 0.0).then_inc(consts_set, 1)
            pool.wait_ge(consts_set, 2)

            def low_half(lo, f, hi, done):
                nc.gpsimd.tensor_tensor(lo, f, hi.bitcast(F32), ALU.subtract).then_inc(done, 1)

            def ffn_rstd(T):
                pool.wait_ge(var_done, ln_count(T))
                nc.gpsimd.tensor_tensor(neg_mean[:], mv[:, 0:NB, 0], neg_one[:], ALU.mult).then_inc(neg_mean_done, 1)
                nc.gpsimd.tensor_tensor(rstd[:, 0:NB], var_eps[:, 0:NB], neg_half[:, 0:NB],
                                        ALU.pow).then_inc(rstd_done, 1)
                pool.wait_ge(neg_mean_done, ln_count(T))
                pool.wait_ge(rstd_done, ln_count(T))
                nc.gpsimd.tensor_tensor(neg_shift[:], neg_mean[:], rstd[:, 0:NB], ALU.mult).then_inc(neg_shift_done, 1)

            def ffn_tile(T, q, last=False, base=TILES):
                for j in range(UNITS):
                    g, k = (q + j) % 2, j % 3
                    if j == 0:
                        wait(pool, h_lo_done, UNITS * T)
                    elif j == PAIRS:
                        pool.wait_ge(h_lo_done, UNITS * T + j)
                    pool.wait_ge(h_hi_done, UNITS * T + j + 1)
                    if j < PAIRS:
                        low_half(h_l[k][:], h[g], h_h[k][:], h_lo_done)
                    else:
                        low_half(h_h[k][INTER:P, :], h[g][0:INTER, :], h_h[k][0:INTER, :], h_lo_done)
                    if j == 2 and not last:
                        ffn_rstd(T + 2)
                    elif j == 2 and base == 0:
                        pool.wait_ge(xn_done, TILES + 1)
                        attn_rstd(0)

            def ffn(base):
                ffn_phase(base)
                ffn_rstd(base)
                ffn_rstd(base + 1)
                if base == 0:
                    pool.wait_ge(w13_hi[1], 1)
                    low_half(w13_l[:, early[1], :], w13_f[:, early[1], :], w13_h[:, early[1], :], w13_split[1])
                    pool.wait_ge(w2_hi, 1)
                    low_half(w2_l[:], w2_f, w2_h[:], w2_split)
                ffn_tile(base, 0)
                if base == 0:
                    pool.wait_ge(h_lo_done, UNITS)
                    pool.wait_ge(wqkv_hi, 1)
                    low_half(wqkv_l[:], wqkv_f, wqkv_h[:], wqkv_split)
                with pool.Fori(0, TILES // 2 - 1) as k:
                    ffn_tile(base + 2 * k + 1, 1)
                    ffn_tile(base + 2 * k + 2, 0)
                ffn_tile(base + TILES - 1, 1, True, base)
                pool.wait_ge(h_lo_done, UNITS * (base + TILES))

            def attn_rstd(b):
                pool.wait_ge(a_var_done, b + 1)
                nc.gpsimd.tensor_tensor(rstd[:], var_eps[:], neg_half[:], ALU.pow).then_inc(a_rstd_done, 1)

            def rope_sin(b, p, n):
                s = n % ROPE_BUFS
                pool.wait_ge(qkv_done, QB * b + n + 1)
                wait(pool, rot_done, QB * b + n - ROPE_BUFS + 1)
                src = qkv[p][:, n, 0:2 * D].rearrange("p (w i e) -> p w i e", w=2, e=2)[:, :, :, ::-1]
                nc.gpsimd.tensor_tensor(rope_s[s][:].rearrange("p w (i e) -> p w i e", e=2), src,
                                        sin[:, n, :, :].rearrange("p w (i e) -> p w i e", e=2),
                                        ALU.mult).then_inc(rope_s_done, 1)

            def attn_prep(b, p, first=False):
                for n in range(QB):
                    rope_sin(b, p, n)
                    if n == (NB + 1 if first else QB - 1):
                        attn_rstd(b + 1)

            ffn(0)
            pool.wait_ge(attn_loaded, 16 * 4)
            attn_prep(0, 0, True)
            with pool.Fori(0, B // 2 - 1) as k:
                attn_prep(2 * k + 1, 1)
                attn_prep(2 * k + 2, 0)
            attn_prep(B - 1, 1)
            ffn(TILES)

        @block.scalar
        def _(act):
            def copy(dst, src):
                return nc.scalar.activation(dst, src, ACT.Copy)

            def ffn_xn(T, Tx, n):
                if n == 0:
                    act.wait_ge(neg_shift_done, ln_count(T))
                    wait(act, xnT_ready, T)
                ins = nc.scalar.activation(xn[:, n, :], X[:, bass.ds(NB * Tx + n, 1), :].rearrange("p a d -> p (a d)"),
                                           ACT.Identity, bias=neg_shift[:, n:n + 1], scale=rstd[:, n:n + 1])
                if n == NB - 1:
                    ins.then_inc(xn_done, 1)

            def ffn_xh(T, q):
                act.wait_ge(xnT_ready, T + 1)
                copy(xh[q][:], bank[:, T_BANK, :]).then_inc(xh_done, 1)

            def ffn_gsilu(T):
                act.wait_ge(route_step, ROUTE * T + 4)
                nc.scalar.activation(gsilu[:], logit[:], ACT.Silu).then_inc(gsilu_done, 1)

            def ffn_combT(T, q):
                act.wait_ge(combT_ready, T + 1)
                wait(act, comb_written, 16 * (T - 1))
                copy(combT[q][:], bank[0:NEXP * NB, T_BANK, 0:P]).then_inc(combT_done, 1)

            def ffn_silu(T, q, j):
                g = (q + j) % 2
                rows = P if j < PAIRS else INTER
                act.wait_ge(gate_ready, UNITS * T + j + 1)
                if j >= 2:
                    act.wait_ge(weighted_done, PAIRS * T + j - 1)
                elif j == 1:
                    wait(act, h_done, UNITS * T)
                else:
                    wait(act, weighted_done, PAIRS * T)
                nc.scalar.activation(silu[g][0:rows, :], bank[0:rows, G_BANK[g], :], ACT.Silu).then_inc(silu_done, 1)

            def ffn_h_hi(T, q, j):
                rows = P if j < PAIRS else INTER
                act.wait_ge(h_done, UNITS * T + j + 1)
                wait(act, down_done, UNITS * T + j - 2)
                copy(h_h[j % 3][0:rows, :], h[(q + j) % 2][0:rows, :]).then_inc(h_hi_done, 1)

            def ffn_yT(T, q):
                act.wait_ge(down_done, UNITS * (T + 1))
                wait(act, y_ready, T)
                copy(yT, bank[:, Y_BANK[q], :]).then_inc(yT_done, 1)

            def ffn_tile(T, Tx, q, first, last, attn_next=False):
                for j in range(UNITS):
                    if j == 0 and not last:
                        ffn_xh(T + 1, 1 - q)
                    if j == 6 and not last:
                        ffn_combT(T + 1, 1 - q)
                    ffn_silu(T, q, j)
                    if j >= 1:
                        ffn_h_hi(T, q, j - 1)
                    elif not first:
                        ffn_h_hi(T - 1, 1 - q, UNITS - 1)
                    if j == 2 and not last:
                        ffn_gsilu(T + 1)
                    if j == LAG and not first:
                        ffn_yT(T - 1, 1 - q)
                    if j >= UNITS - 1 - NB and j < UNITS - 1 and not last:
                        ffn_xn(T + 2, Tx + 2, j - (UNITS - 1 - NB))
                    if attn_next and TAIL_UNIT < j:
                        attn_item(ITEMS[j - 1 - TAIL_UNIT], 0, 0, True)

            def ffn(base):
                start = base == 0
                if start:
                    ffn_phase(base)
                    act.wait_ge(gate_loaded, 16 * 3)
                    copy(gw_hl[:, 0:NEXP], gw_f[:]).then_inc(gw_hi, 1)
                    act.wait_ge(w13_loaded[0], 16)
                    copy(w13_h[:, early[0], :], w13_f[:, early[0], :]).then_inc(w13_hi[0], 1)
                    for n in range(NB):
                        ffn_xn(base, 0, n)
                    ffn_xh(base, 0)
                    act.wait_ge(w13_loaded[1], 16)
                    copy(w13_h[:, early[1], :], w13_f[:, early[1], :]).then_inc(w13_hi[1], 1)
                    ffn_gsilu(base)
                    for n in range(NB):
                        ffn_xn(base + 1, 1, n)
                    act.wait_ge(w2_loaded, 16)
                    copy(w2_h[:], w2_f).then_inc(w2_hi, 1)
                    ffn_combT(base, 0)
                ffn_tile(base, 0, 0, True, False)
                if start:
                    act.wait_ge(attn_loaded, 16 * 4)
                    copy(wqkv_h[:], wqkv_f).then_inc(wqkv_hi, 1)
                    copy(mask[:], mask_f).then_inc(consts_rounded, 1)
                    copy(ident_r[:], ident[:]).then_inc(consts_rounded, 1)
                with act.Fori(0, TILES // 2 - 1) as k:
                    ffn_tile(base + 2 * k + 1, 2 * k + 1, 1, False, False)
                    ffn_tile(base + 2 * k + 2, 2 * k + 2, 0, False, False)
                T = base + TILES - 1
                ffn_tile(T, TILES - 1, 1, False, True, start)
                ffn_h_hi(T, 1, UNITS - 1)
                if start:
                    for item in TAIL_ITEMS[-1:] + NEXT_ITEMS[:2]:
                        attn_item(item, 0, 0, True)
                ffn_yT(T, 1)

            def attn_item(item, b, p, prologue=False):
                kind, n = item
                m = m_bank(item, prologue)
                if kind == "xnT":
                    act.wait_ge(a_xnT_ready, 2 * b + n + 1)
                    copy(xh_half[n][:], bank[:, m, :]).then_inc(a_xh_done, 1)
                elif kind == "qkv":
                    act.wait_ge(qkv_ready, QB * b + n + 1)
                    copy(qkv[p][:, n, :], bank[:, m, 0:3 * D]).then_inc(qkv_done, 1)
                else:
                    act.wait_ge(qkT_ready, QB // 2 * b + n + 1)
                    copy(qkT_h[p][:, :, 2 * P * n:2 * P * (n + 1)],
                         bank[:, m, :].rearrange("p (w c) -> p w c", w=2)).then_inc(qkT_h_done, 1)

            def attn_exp(b, p, i):
                s, w = i % 2, (i + 1) * P
                act.wait_ge(negmax_done, QB * b + i + 1)
                if i >= 2:
                    act.wait_ge(probT_ready, PT_CHUNKS * b + chunk_index(i - 2, 1) + 1)
                else:
                    wait(act, probT_ready, PT_CHUNKS * (b - 1) + chunk_index(QB - 2 + i, 1) + 1)
                nc.scalar.activation(prob[s][:, 0:w],
                                     bank[:, 2 * s:2 * s + 2, :].rearrange("p a c -> p (a c)")[:, 0:w],
                                     ACT.Exp, bias=negmax[s][:],
                                     accum_out=rowsum[p][:, i:i + 1]).then_inc(exp_done, 1)

            def attn_probT(b, i, c, last):
                s, m = i % 2, chunk_index(i, c)
                blocks = min(4, i + 1 - 4 * c)
                act.wait_ge(probT_ready, PT_CHUNKS * b + m + 1)
                if c == 0 and i >= 2:
                    act.wait_ge(pv_ready, QB * b + i - 1)
                elif c == 0:
                    wait(act, pv_ready, QB * (b - 1) + QB - 1 + i)
                copy(probT[s][:, 4 * c:4 * c + blocks, :].rearrange("p a c -> p (a c)"),
                     bank[:, probT_bank(i, c, last), 0:blocks * P]).then_inc(probT_done, 1)

            def ffn_prep(i):
                T = TILES
                if i == 1:
                    ffn_phase(T)
                    act.wait_ge(a_xn_done, 2 * (B + 1))
                    for n in range(NB):
                        ffn_xn(T, 0, n)
                elif i == 2:
                    ffn_xh(T, 0)
                elif i == 4:
                    ffn_gsilu(T)
                elif i == 6:
                    ffn_combT(T, 0)
                elif i == 7:
                    for n in range(NB):
                        ffn_xn(T + 1, 1, n)

            def attn_batch(b, p, last):
                for i in range(QB):
                    before, after = ([], []) if last else step_items(i)
                    if i >= 1:
                        attn_probT(b, i, 0, last)
                    for item in before:
                        attn_item(item, b + 1, 1 - p)
                    if i == 0:
                        attn_probT(b, i, 0, last)
                    if i >= NB:
                        attn_probT(b, i, 1, last)
                    if i + 1 < QB:
                        attn_exp(b, p, i + 1)
                    elif not last:
                        attn_exp(b + 1, 1 - p, 0)
                    for item in after:
                        attn_item(item, b + 1, 1 - p)
                    if last:
                        ffn_prep(i)

            ffn(0)
            for item in NEXT_ITEMS[2:]:
                attn_item(item, 0, 0, True)
            attn_exp(0, 0, 0)
            attn_batch(0, 0, False)
            with act.Fori(0, B // 2 - 1) as k:
                attn_batch(2 * k + 1, 1, False)
                attn_batch(2 * k + 2, 0, False)
            attn_batch(B - 1, 1, True)
            ffn(TILES)

        @block.vector
        def _(dve):
            def low_half(lo, f, hi, done):
                nc.vector.tensor_tensor(lo, f, hi.bitcast(F32), ALU.subtract).then_inc(done, 1)

            def ln_stats(blocks, first_block, done, at=0):
                for n in range(blocks):
                    ins = nc.vector.bn_stats(stats[:, at + n, :], X[:, bass.ds(first_block + n, 1), :].rearrange("p a d -> p (a d)"))
                ins.then_inc(done, 1)

            def ln_mean_var(blocks, count, mv_sem, var_sem):
                for n in range(blocks):
                    ins = nc.vector.bn_aggr(mv[:, n, :], stats[:, n, :])
                ins.then_inc(mv_sem, 1)
                dve.wait_ge(mv_sem, count)
                nc.vector.tensor_scalar_add(var_eps[:, 0:blocks], mv[:, 0:blocks, 1], EPS).then_inc(var_sem, 1)

            def ln_apply(blocks, first_block, done, at=0):
                for n in range(at, at + blocks):
                    ins = nc.vector.tensor_scalar(xn[:, n, :], X[:, bass.ds(first_block + n - at, 1), :].rearrange("p a d -> p (a d)"),
                                                  mv[:, n, 0:1], rstd[:, n:n + 1], ALU.subtract, ALU.mult)
                ins.then_inc(done, 1)

            def ffn_xl(T, q):
                dve.wait_ge(xh_done, T + 1)
                nc.vector.tensor_tensor(xl[q][:], bank[:, T_BANK, :], xh[q][:].bitcast(F32),
                                        ALU.subtract).then_inc(xl_done, 1)

            def ffn_logit0(T):
                dve.wait_ge(logits_ready, T + 1)
                nc.vector.reduce_sum(logit0[:], bank[:, T_BANK, 0:NB * 2 * NEXP].rearrange("p (n a e) -> p n e a", n=NB, a=2),
                                     AX_X).then_inc(route_step, 1)

            def ffn_clamp(T):
                dve.wait_ge(route_step, ROUTE * T + 1)
                nc.vector.tensor_scalar(near0[:], logit0[:], -TINY, TINY, ALU.max, ALU.min).then_inc(route_step, 1)

            def ffn_near0(T):
                dve.wait_ge(route_step, ROUTE * T + 2)
                nc.vector.tensor_tensor(near0[:], near0[:], logit0[:], ALU.is_equal).then_inc(route_step, 1)

            def ffn_logit(T):
                dve.wait_ge(route_step, ROUTE * T + 3)
                nc.vector.scalar_tensor_tensor(logit[:], near0[:], 2 * TINY, logit0[:], ALU.mult, ALU.add).then_inc(route_step, 1)

            def ffn_recip(T):
                dve.wait_ge(route_step, ROUTE * T + 4)
                nc.vector.reciprocal(rlogit[:], logit[:]).then_inc(route_step, 1)

            def ffn_score(T):
                dve.wait_ge(gsilu_done, T + 1)
                dve.wait_ge(route_step, ROUTE * T + 5)
                nc.vector.tensor_tensor(score[:], gsilu[:], rlogit[:], ALU.mult).then_inc(route_step, 1)

            def ffn_bias(T):
                dve.wait_ge(route_step, ROUTE * T + 6)
                nc.vector.tensor_tensor(biased[:, :, 0:NEXP], score[:],
                                        gb[:].rearrange("p (a e) -> p a e", a=1).to_broadcast([P, NB, NEXP]),
                                        ALU.add).then_inc(route_step, 1)

            def ffn_biased(T):
                dve.wait_ge(route_step, ROUTE * T + 7)

            def ffn_max(T):
                for n in range(NB):
                    ins = nc.vector.max(top8[:, n, :], biased[:, n, 0:NEXP])
                ins.then_inc(route_step, 1)

            def ffn_top(T):
                dve.wait_ge(route_step, ROUTE * T + 8)
                nc.vector.tensor_copy(take[:, :, 0:TOPK], top8[:, :, 0:TOPK]).then_inc(route_step, 1)

            def ffn_take(T):
                dve.wait_ge(route_step, ROUTE * T + 9)

            def ffn_mark(T):
                for n in range(NB):
                    ins = nc.vector.match_replace(marked[:, n, :], take[:, n, :], biased[:, n, :], TAKEN)
                ins.then_inc(route_step, 1)

            def ffn_chosen(T):
                dve.wait_ge(route_step, ROUTE * T + 10)
                nc.vector.tensor_tensor(chosen[:], marked[:, :, 0:NEXP], biased[:, :, 0:NEXP],
                                        ALU.not_equal).then_inc(route_step, 1)

            def ffn_wsel(T):
                dve.wait_ge(route_step, ROUTE * T + 11)
                nc.vector.tensor_tensor(wsel[:], score[:], chosen[:], ALU.mult).then_inc(route_step, 1)

            def ffn_wsum(T):
                dve.wait_ge(route_step, ROUTE * T + 12)
                nc.vector.reduce_sum(wsum[:], wsel[:], AX_X).then_inc(route_step, 1)

            def ffn_rsum(T):
                dve.wait_ge(route_step, ROUTE * T + 13)
                nc.vector.reciprocal(rsum[:], wsum[:]).then_inc(route_step, 1)

            def ffn_comb(T):
                dve.wait_ge(route_step, ROUTE * T + 14)
                wait(dve, combT_ready, T)
                nc.vector.scalar_tensor_tensor(comb[:, 0:NEXP, :].rearrange("p e n -> p n e"), wsel[:], ROUTE_SCALE,
                                               rsum[:].rearrange("p (n e) -> p n e", e=1).to_broadcast([P, NB, NEXP]),
                                               ALU.mult, ALU.mult).then_inc(route_step, 1)

            def ffn_weighted(T, q, j):
                dve.wait_ge(silu_done, UNITS * T + j + 1)
                dve.wait_ge(comb_loaded[j * COMB_LOADS // PAIRS], 32 * (T + 1))
                nc.vector.tensor_tensor(weighted[j % 2], silu[(q + j) % 2], comb_b[q][:, j, :], ALU.mult).then_inc(weighted_done, 1)

            def ffn_h(T, q, j):
                g = (q + j) % 2
                wait(dve, h_lo_done, UNITS * T + j - 1)
                if j < PAIRS:
                    dve.wait_ge(weighted_done, PAIRS * T + j + 1)
                    dve.wait_ge(up_ready, PAIRS * T + j + 1)
                    nc.vector.tensor_tensor(h[g], weighted[j % 2], bank[:, U_BANK[j % 2], :], ALU.mult).then_inc(h_done, 1)
                else:
                    dve.wait_ge(silu_done, UNITS * T + j + 1)
                    nc.vector.tensor_tensor(h[g][0:INTER, :], silu[g][0:INTER, :], bank[INTER:P, G_BANK[g], :],
                                            ALU.mult).then_inc(h_done, 1)

            def ffn_stats(T, Tx, n):
                ins = nc.vector.bn_stats(stats[:, n, :], X[:, bass.ds(NB * Tx + n, 1), :].rearrange("p a d -> p (a d)"))
                if n == NB - 1:
                    ins.then_inc(stats_done, 1)

            def ffn_stats_wait(T):
                dve.wait_ge(stats_done, ln_count(T))

            def ffn_mv(T):
                for n in range(NB):
                    ins = nc.vector.bn_aggr(mv[:, n, :], stats[:, n, :])
                ins.then_inc(mv_done, 1)

            def ffn_var(T):
                dve.wait_ge(mv_done, ln_count(T))
                nc.vector.tensor_scalar_add(var_eps[:, 0:NB], mv[:, 0:NB, 1], EPS).then_inc(var_done, 1)

            def residual(T, Tx):
                dve.wait_ge(y_ready, T + 1)
                xt = X[:, tile_blocks(Tx), :]
                nc.vector.scalar_tensor_tensor(xt, bank[:, YT_BANK, :].rearrange("p (n d) -> p n d", n=NB), 0.5, xt,
                                               ALU.mult, ALU.add).then_inc(x_done, 1)

            def ffn_tile(T, Tx, q, first, last, attn_next=False):
                N, L, Lx = T + 1, T + 2, Tx + 2
                if last:
                    for j in range(PAIRS):
                        ffn_weighted(T, q, j)
                        if j == 7 and not first:
                            residual(T - 1, Tx - 1)
                        ffn_h(T, q, j)
                        if attn_next:
                            attn_start(j)
                    ffn_h(T, q, PAIRS)
                    return
                ffn_xl(N, 1 - q)
                ffn_weighted(T, q, 0)
                ffn_stats(L, Lx, 0)
                ffn_h(T, q, 0)
                ffn_stats(L, Lx, 1)
                ffn_logit0(N)
                ffn_weighted(T, q, 1)
                ffn_clamp(N)
                ffn_h(T, q, 1)
                ffn_near0(N)
                ffn_stats(L, Lx, 2)
                ffn_stats(L, Lx, 3)
                ffn_logit(N)
                ffn_stats_wait(L)
                ffn_weighted(T, q, 2)
                ffn_mv(L)
                ffn_recip(N)
                ffn_h(T, q, 2)
                ffn_score(N)
                ffn_var(L)
                ffn_bias(N)
                ffn_biased(N)
                ffn_weighted(T, q, 3)
                ffn_max(N)
                ffn_h(T, q, 3)
                ffn_top(N)
                ffn_take(N)
                ffn_weighted(T, q, 4)
                ffn_mark(N)
                ffn_h(T, q, 4)
                ffn_chosen(N)
                ffn_wsel(N)
                ffn_wsum(N)
                ffn_rsum(N)
                ffn_comb(N)
                for j in (5, 6):
                    ffn_weighted(T, q, j)
                    ffn_h(T, q, j)
                ffn_weighted(T, q, 7)
                if not first:
                    residual(T - 1, Tx - 1)
                ffn_h(T, q, 7)
                ffn_h(T, q, 8)

            def ffn_start():
                ffn_phase(0)
                dve.wait_ge(x_loaded[0], 16)
                for n in range(NB):
                    ffn_stats(0, 0, n)
                ffn_stats_wait(0)
                ffn_mv(0)
                ffn_var(0)
                dve.wait_ge(gw_hi, 1)
                low_half(gw_hl[:, NEXP:2 * NEXP], gw_f[:], gw_hl[:, 0:NEXP], gw_split)
                dve.wait_ge(w13_hi[0], 1)
                low_half(w13_l[:, early[0], :], w13_f[:, early[0], :], w13_h[:, early[0], :], w13_split[0])
                ffn_xl(0, 0)
                dve.wait_ge(x_loaded[1], 16)
                for n in range(NB):
                    ffn_stats(1, 1, n)
                ffn_logit0(0)
                ffn_clamp(0)
                ffn_stats_wait(1)
                ffn_near0(0)
                ffn_mv(1)
                ffn_logit(0)
                ffn_var(1)
                ffn_recip(0)
                dve.wait_ge(consts_set, 6)
                ffn_score(0)
                ffn_bias(0)
                ffn_top4(0)
                ffn_weights(0)

            def ffn_top4(T):
                ffn_biased(T)
                ffn_max(T)
                ffn_top(T)
                ffn_take(T)
                ffn_mark(T)

            def ffn_weights(T):
                ffn_chosen(T)
                ffn_wsel(T)
                ffn_wsum(T)
                ffn_rsum(T)
                ffn_comb(T)

            def ffn(base):
                start = base == 0
                if start:
                    ffn_start()
                ffn_tile(base, 0, 0, True, False)
                if start:
                    dve.wait_ge(x_loaded[2], 16)
                with dve.Fori(0, TILES // 2 - 1) as k:
                    ffn_tile(base + 2 * k + 1, 2 * k + 1, 1, False, False)
                    ffn_tile(base + 2 * k + 2, 2 * k + 2, 0, False, False)
                ffn_tile(base + TILES - 1, TILES - 1, 1, False, True, start)
                if start:
                    attn_start_tail()
                residual(base + TILES - 1, TILES - 1)

            def rope_add(b, n):
                s = n % ROPE_BUFS
                dve.wait_ge(rope_c_done, QB * b + n + 1)
                dve.wait_ge(rope_s_done, QB * b + n + 1)
                wait(dve, qkT_ready, QB // 2 * b + (n - ROPE_BUFS) // 2 + 1)
                nc.vector.tensor_tensor(rot[s][:], rope_c[s][:], rope_s[s][:], ALU.add).then_inc(rot_done, 1)

            def attn_item(item, b, p, prologue=False):
                kind, n = item
                m = m_bank(item, prologue)
                if kind == "xnT":
                    dve.wait_ge(a_xh_done, 2 * b + n + 1)
                    nc.vector.tensor_tensor(xl_half[n][:], bank[:, m, :], xh_half[n][:].bitcast(F32),
                                            ALU.subtract).then_inc(a_xl_done, 1)
                elif kind == "qkv":
                    s = n % ROPE_BUFS
                    dve.wait_ge(qkv_done, QB * b + n + 1)
                    nc.vector.tensor_tensor(rope_c[s][:], qkv[p][:, n, 0:2 * D].rearrange("p (w d) -> p w d", w=2),
                                            cos[:, n, :, :], ALU.mult).then_inc(rope_c_done, 1)
                    if n >= 1:
                        rope_add(b, n - 1)
                else:
                    if n == QB // 2 - 2:
                        rope_add(b, QB - 1)
                    dve.wait_ge(qkT_h_done, QB // 2 * b + n + 1)
                    cols = slice(2 * P * n, 2 * P * (n + 1))
                    nc.vector.tensor_tensor(qkT_l[p][:, :, cols], bank[:, m, :].rearrange("p (w c) -> p w c", w=2),
                                            qkT_h[p][:, :, cols].bitcast(F32), ALU.subtract).then_inc(qkT_l_done, 1)

            def attn_max(b, i):
                s, w = i % 2, (i + 1) * P
                wait(dve, exp_done, QB * b + i - 1)
                dve.wait_ge(scores_ready, QB * b + i + 1)
                nc.vector.reduce_max(negmax[s][:], bank[:, 2 * s:2 * s + 2, :].rearrange("p a c -> p (a c)")[:, 0:w],
                                     AX_X, negate=True).then_inc(negmax_done, 1)

            def attn_rrow(b, p, i):
                dve.wait_ge(exp_done, QB * b + i + 1)
                nc.vector.reciprocal(rrow[p][:, i:i + 1], rowsum[p][:, i:i + 1]).then_inc(rrow_done, 1)

            def attn_residual(b, p, i):
                dve.wait_ge(rrow_done, QB * b + i + 1)
                dve.wait_ge(pv_ready, QB * b + i + 1)
                xb = X[:, bass.ds(QB * b + i, 1), :].rearrange("p a d -> p (a d)")
                nc.vector.scalar_tensor_tensor(xb, bank[:, O_BANK, 0:D], rrow[p][:, i:i + 1], xb,
                                               ALU.mult, ALU.add).then_inc(attn_done, 1)

            def attn_stats(b):
                dve.wait_ge(a_stats_done, 2 * b + 2)

            def attn_ln(b, part):
                if part < 2:
                    ln_stats(NB, QB * b + NB * part, a_stats_done, NB * part)
                elif part == 2:
                    ln_mean_var(QB, b + 1, a_mv_done, a_var_done)
                else:
                    half = part - 3
                    dve.wait_ge(a_rstd_done, b + 1)
                    wait(dve, a_xnT_ready, 2 * (b - 1) + half + 1)
                    ln_apply(NB, QB * b + NB * half, a_xn_done, NB * half)

            def ffn_prep(i):
                T = TILES
                if i == 0:
                    ffn_phase(T)
                    for n in range(NB):
                        ffn_stats(T, 0, n)
                    ffn_stats_wait(T)
                    ffn_mv(T)
                    ffn_var(T)
                elif i == 3:
                    ffn_xl(T, 0)
                    for n in range(NB):
                        ffn_stats(T + 1, 1, n)
                    ffn_stats_wait(T + 1)
                elif i == 4:
                    ffn_logit0(T)
                    ffn_clamp(T)
                    ffn_mv(T + 1)
                    ffn_near0(T)
                    ffn_var(T + 1)
                    ffn_logit(T)
                    ffn_recip(T)
                elif i == 5:
                    ffn_score(T)
                    ffn_bias(T)
                    ffn_top4(T)
                elif i == 6:
                    ffn_weights(T)

            def attn_start(j):
                if j < 2:
                    attn_ln(0, j)
                elif j == 2:
                    attn_stats(0)
                    attn_ln(0, 2)
                elif 3 < j <= TAIL_UNIT:
                    attn_ln(0, j - 1)
                elif j > TAIL_UNIT:
                    attn_item(ITEMS[j - 1 - TAIL_UNIT], 0, 0, True)

            def attn_start_tail():
                dve.wait_ge(attn_loaded, 16 * 4)
                attn_item(TAIL_ITEMS[-2], 0, 0, True)
                attn_ln(1, 0)
                attn_item(TAIL_ITEMS[-1], 0, 0, True)
                attn_item(NEXT_ITEMS[0], 0, 0, True)
                attn_ln(1, 1)
                attn_stats(1)
                attn_item(NEXT_ITEMS[1], 0, 0, True)

            def attn_batch(b, p, first, last):
                for i in range(QB):
                    if i == 5 and not last:
                        attn_stats(b + 2)
                    if i + 1 < QB:
                        attn_max(b, i + 1)
                    elif not last:
                        attn_max(b + 1, 0)
                    if last and i == 0:
                        ffn_prep(i)
                    if i >= 1:
                        attn_residual(b, p, i - 1)
                    elif not first:
                        attn_residual(b - 1, 1 - p, QB - 1)
                    attn_rrow(b, p, i)
                    if last and i >= 1:
                        ffn_prep(i)
                    elif not last:
                        for item in sum(step_items(i), []):
                            attn_item(item, b + 1, 1 - p)
                        if i >= 3:
                            attn_ln(b + 2, i - 3)

            ffn(0)
            for item in NEXT_ITEMS[2:6]:
                attn_item(item, 0, 0, True)
            attn_ln(1, 2)
            for item in NEXT_ITEMS[6:]:
                attn_item(item, 0, 0, True)
            attn_max(0, 0)
            attn_ln(1, 3)
            attn_ln(1, 4)
            attn_batch(0, 0, True, False)
            with dve.Fori(0, B // 2 - 1) as k:
                attn_batch(2 * k + 1, 1, False, False)
                attn_batch(2 * k + 2, 0, False, False)
            attn_batch(B - 1, 1, False, True)
            attn_residual(B - 1, 1, QB - 1)
            ffn(TILES)

        @block.tensor
        def _(pe):
            def mm(dst, lhsT, rhs, start, stop):
                return nc.tensor.matmul(dst, lhsT, rhs, start=start, stop=stop)

            def mm3(dst, lh, ll, rh, rl, start=True, stop=True):
                mm(dst, lh, rh, start, False)
                mm(dst, lh, rl, False, False)
                return mm(dst, ll, rh, False, stop)

            def ffn_xnT(T):
                pe.wait_ge(xn_done, ln_count(T))
                wait(pe, combT_done, T)
                for n in range(NB):
                    ins = nc.tensor.transpose(bank[:, T_BANK, n * P:(n + 1) * P], xn[:, n, :], ident[:])
                ins.then_inc(xnT_ready, 1)

            def ffn_logits(T, q):
                pe.wait_ge(xl_done, T + 1)
                for n in range(NB):
                    blk, at = slice(n * P, (n + 1) * P), 2 * NEXP * n
                    mm(bank[:, T_BANK, at:at + 2 * NEXP], xh[q][:, blk], gw_hl[:], True, False)
                    ins = mm(bank[:, T_BANK, at:at + NEXP], xl[q][:, blk], gw_hl[:, 0:NEXP], False, True)
                ins.then_inc(logits_ready, 1)

            def ffn_combT(T):
                pe.wait_ge(route_step, ROUTE * (T + 1))
                nc.tensor.transpose(bank[:, T_BANK, 0:P], comb[:].rearrange("p e n -> p (e n)"),
                                    ident[:]).then_inc(combT_ready, 1)

            def ffn_y(T):
                pe.wait_ge(yT_done, T + 1)
                wait(pe, x_done, T)
                for n in range(NB):
                    ins = nc.tensor.transpose(bank[:, YT_BANK, n * P:(n + 1) * P], yT[:, n * P:(n + 1) * P], ident[:])
                ins.then_inc(y_ready, 1)

            def ffn_up(T, q, j, T_next):
                g, c = (q + j) % 2, j % 2
                if j == 1:
                    wait(pe, h_done, UNITS * T)
                else:
                    wait(pe, silu_done, UNITS * T + j - 1)
                mm3(bank[:, G_BANK[g], :], w13_h[:, 2 * j, :], w13_l[:, 2 * j, :], xh[q][:], xl[q][:]).then_inc(gate_ready, 1)
                if j == 1 and T_next is not None:
                    ffn_logits(T_next, 1 - q)
                if j < PAIRS:
                    if j >= 2:
                        pe.wait_ge(h_done, UNITS * T + j - 1)
                    else:
                        wait(pe, h_done, UNITS * (T - 1) + PAIRS - 1 + j)
                    mm3(bank[:, U_BANK[c], :], w13_h[:, 2 * j + 1, :], w13_l[:, 2 * j + 1, :],
                        xh[q][:], xl[q][:]).then_inc(up_ready, 1)

            def ffn_down(T, q, j):
                pe.wait_ge(h_lo_done, UNITS * T + j + 1)
                if j == 0:
                    wait(pe, yT_done, T - 1)
                Y, k = bank[:, Y_BANK[q], :], j % 3
                if j < PAIRS:
                    mm(Y, w2_h[:, j, :], h_h[k][:], j == 0, False)
                    mm(Y, w2_l[:, j, :], h_h[k][:], False, False)
                    ins = mm(Y, w2_h[:, j, :], h_l[k][:], False, False)
                else:
                    mm(Y, w2_h[:, j, :], h_h[k][:], False, False)
                    ins = mm(Y, w2_l[:, j, :], h_h[k][:], False, True)
                ins.then_inc(down_done, 1)

            def ffn_tile(T, q, first, last, start, attn_next=False):
                if not start and not last:
                    ffn_xnT(T + 1)
                for j in range(UNITS):
                    if start and j == EARLY:
                        pe.wait_ge(w13_split[1], 1)
                        pe.wait_ge(w2_split, 1)
                    ffn_up(T, q, j, None if last else T + 1)
                    if start and j == 0:
                        ffn_combT(T)
                        ffn_xnT(T + 1)
                    if j == 6 and not last:
                        ffn_combT(T + 1)
                    if j >= LAG:
                        ffn_down(T, q, j - LAG)
                    elif not first:
                        ffn_down(T - 1, 1 - q, UNITS - LAG + j)
                    if attn_next and j >= TAIL_UNIT:
                        attn_item(ITEMS[j - TAIL_UNIT], 0, 0, True)
                    if j == 4 and not first:
                        ffn_y(T - 1)

            def ffn(base):
                start = base == 0
                if start:
                    ffn_phase(base)
                    pe.wait_ge(gate_loaded, 16 * 3)
                    ffn_xnT(base)
                    pe.wait_ge(gw_split, 1)
                    ffn_logits(base, 0)
                    pe.wait_ge(w13_split[0], 1)
                ffn_tile(base, 0, True, False, start)
                with pe.Fori(0, TILES // 2 - 1) as k:
                    ffn_tile(base + 2 * k + 1, 1, False, False, False)
                    ffn_tile(base + 2 * k + 2, 0, False, False, False)
                T = base + TILES - 1
                if start:
                    pe.wait_ge(wqkv_split, 1)
                    pe.wait_ge(consts_rounded, 2)
                ffn_tile(T, 1, False, True, False, start)
                for j in range(UNITS - LAG, UNITS):
                    ffn_down(T, 1, j)
                    if start:
                        attn_item(NEXT_ITEMS[j - UNITS + LAG], 0, 0, True)
                ffn_y(T)

            def attn_item(item, b, p, prologue=False):
                kind, n = item
                order = ITEMS if prologue else SLOTS
                at, m = order.index(item), m_bank(item, prologue)
                kind2, n2 = order[at - 2]
                row = b if at >= 2 else b - 1
                if prologue and at == 0:
                    pe.wait_ge(yT_done, TILES - 1)
                elif prologue and at == 1:
                    pe.wait_ge(combT_done, TILES)
                elif at < 2 and isinstance(b, int) and b == 1:
                    pe.wait_ge(qkT_l_done, QB // 2)
                elif kind2 == "xnT":
                    pe.wait_ge(a_xl_done, 2 * row + n2 + 1)
                elif kind2 == "qkv":
                    wait(pe, qkv_done, QB * row + n2 + 1)
                elif kind2 == "qkT":
                    wait(pe, qkT_l_done, QB // 2 * row + n2 + 1)
                else:
                    wait(pe, probT_done, PT_CHUNKS * (row - 1) + chunk_index(n2, 1) + 1)
                if kind == "xnT":
                    pe.wait_ge(a_xn_done, 2 * b + n + 1)
                    for a in range(NB):
                        ins = nc.tensor.transpose(bank[:, m, a * P:(a + 1) * P], xn[:, NB * n + a, :], ident[:])
                    ins.then_inc(a_xnT_ready, 1)
                elif kind == "qkv":
                    a, blk = n // NB, slice(n % NB * P, (n % NB + 1) * P)
                    pe.wait_ge(a_xl_done, 2 * b + a + 1)
                    mm3(bank[:, m, 0:3 * D], xh_half[a][:, blk], xl_half[a][:, blk], wqkv_h[:], wqkv_l[:]).then_inc(qkv_ready, 1)
                else:
                    pe.wait_ge(rot_done, QB * b + 2 * n + 2)
                    for a in range(2):
                        for w in range(2):
                            c = w * 2 * P + a * P
                            ins = nc.tensor.transpose(bank[:, m, c:c + P], rot[(2 * n + a) % ROPE_BUFS][:, w, :], ident[:])
                    ins.then_inc(qkT_ready, 1)

            def attn_scores(b, p, i):
                s = i % 2
                pe.wait_ge(qkT_l_done, QB // 2 * b + i // 2 + 1)
                wait(pe, exp_done, QB * b + i - 1)
                qs = slice(i * P, (i + 1) * P)
                for c in range(1 + i // 4):
                    k0, k1 = 512 * c, min(512 * (c + 1), (i + 1) * P)
                    dst = bank[:, 2 * s + c, 0:k1 - k0]
                    diag = c == i // 4
                    ins = mm3(dst, qkT_h[p][:, 0, qs], qkT_l[p][:, 0, qs], qkT_h[p][:, 1, k0:k1], qkT_l[p][:, 1, k0:k1],
                              True, not diag)
                    if diag:
                        ins = mm(bank[:, 2 * s + c, k1 - k0 - P:k1 - k0], ident_r[:], mask[:], False, True)
                ins.then_inc(scores_ready, 1)

            def attn_probT(b, i, c, last):
                s, m = i % 2, chunk_index(i, c)
                if c == 0:
                    pe.wait_ge(exp_done, QB * b + i + 1)
                if c == 0:
                    wait(pe, probT_done, PT_CHUNKS * (b if i else b - 1) + chunk_index((i - 1) % QB, 0) + 1)
                elif last:
                    if i > NB:
                        pe.wait_ge(probT_done, PT_CHUNKS * b + chunk_index(i - 1, 1) + 1)
                else:
                    kind2, n2 = SLOTS[SLOTS.index(("probT", i)) - 2]
                    if kind2 == "qkv":
                        pe.wait_ge(qkv_done, QB * (b + 1) + n2 + 1)
                    elif kind2 == "qkT":
                        pe.wait_ge(qkT_l_done, QB // 2 * (b + 1) + n2 + 1)
                    else:
                        pe.wait_ge(probT_done, PT_CHUNKS * b + chunk_index(n2, 1) + 1)
                blocks = min(4, i + 1 - 4 * c)
                for a in range(blocks):
                    k0 = (4 * c + a) * P
                    ins = nc.tensor.transpose(bank[:, probT_bank(i, c, last), a * P:(a + 1) * P], prob[s][:, k0:k0 + P], ident[:])
                ins.then_inc(probT_ready, 1)

            def attn_pv(b, p, i):
                s = i % 2
                wait(pe, attn_done, QB * b + i)
                for kb in range(i + 1):
                    if kb % 4 == 0:
                        pe.wait_ge(probT_done, PT_CHUNKS * b + chunk_index(i, kb // 4) + 1)
                    ins = mm(bank[:, O_BANK, 0:D], probT[s][:, kb, :], qkv[p][:, kb, 2 * D:3 * D], kb == 0, kb == i)
                ins.then_inc(pv_ready, 1)

            def ffn_prep(i):
                T = TILES
                if i == 3:
                    ffn_phase(T)
                    pe.wait_ge(qkT_l_done, B * QB // 2)
                    ffn_xnT(T)
                elif i == 4:
                    ffn_logits(T, 0)
                elif i == 7:
                    ffn_combT(T)

            def attn_batch(b, p, first, last):
                for i in range(QB):
                    if i + 1 < QB:
                        attn_scores(b, p, i + 1)
                    elif not last:
                        attn_scores(b + 1, 1 - p, 0)
                    before, after = ([], []) if last else step_items(i)
                    if i == 0:
                        for item in before:
                            attn_item(item, b + 1, 1 - p)
                    if i >= 1:
                        attn_pv(b, p, i - 1)
                    elif not first:
                        attn_pv(b - 1, 1 - p, QB - 1)
                    if last:
                        ffn_prep(i)
                    attn_probT(b, i, 0, last)
                    if i >= 1:
                        for item in before:
                            attn_item(item, b + 1, 1 - p)
                    if i >= NB:
                        attn_probT(b, i, 1, last)
                    for item in after:
                        attn_item(item, b + 1, 1 - p)

            ffn(0)
            for item in NEXT_ITEMS[LAG:]:
                attn_item(item, 0, 0, True)
            pe.wait_ge(x_done, TILES)
            attn_scores(0, 0, 0)
            attn_batch(0, 0, True, False)
            with pe.Fori(0, B // 2 - 1) as k:
                attn_batch(2 * k + 1, 1, False, False)
                attn_batch(2 * k + 2, 0, False, False)
            attn_batch(B - 1, 1, False, True)
            attn_pv(B - 1, 1, QB - 1)
            ffn(TILES)


def probT_bank(i, c, last):
    return PT_BANK if c == 0 else M_BANK[0] if last else m_bank(("probT", i))


def chunk_index(i, c):
    c = min(c, i // 4)
    return i if i < 4 else 4 + 2 * (i - 4) + c


def rope_tables():
    f = np.float32
    i = np.arange(D // 2, dtype=f)
    theta = np.power(f(10000.0), (f(-2.0) * (i - f(1.0)) / f(D)).astype(f)).astype(f)
    ang = (np.arange(M, dtype=f)[:, None] * theta[None, :]).astype(f).astype(np.float64)
    c = np.repeat(np.cos(ang).astype(f), 2, axis=1)
    s = np.repeat(np.sin(ang).astype(f), 2, axis=1)
    s[:, 1::2] *= -1
    scale = np.array([SCORE_SCALE, 1.0])[:, None]
    return [(t.reshape(QB, P, 1, D).astype(np.float64) * scale).astype(f).transpose(1, 0, 2, 3) for t in (c, s)]


def kernel(**inputs):
    import concourse.bacc as bacc
    from concourse.bass_utils import run_bass_kernel_spmd

    a = {k: np.asarray(v) for k, v in inputs.items()}
    w13 = a["L0_ffn_w13"].reshape(PAIRS, 2, 2, INTER, D).transpose(4, 0, 2, 1, 3).reshape(D, 2 * PAIRS, P)
    w13T = np.concatenate([w13, a["L0_ffn_w13_s"].T.reshape(D, 1, P)], axis=1)
    w2 = a["L0_ffn_w2"].reshape(PAIRS, 2, D, INTER).transpose(1, 3, 0, 2).reshape(P, PAIRS, D)
    w2s = np.concatenate([a["L0_ffn_w2_s"].T, a["L0_ffn_w2_s"].T], axis=0)
    w2T = np.concatenate([w2, w2s.reshape(P, 1, D)], axis=1)
    wqkvT = np.concatenate([a["L0_attn_w_q"].T, a["L0_attn_w_k"].T, a["L0_attn_w_v"].T], axis=1)
    row, col = np.arange(P)[:, None], np.arange(P)[None, :]
    mask = np.where(col > row, np.float32(MASKED), np.float32(0.0)).astype(np.float32)
    cos, sin = rope_tables()
    arrays = {
        "x": a["L0_attn_x"], "w13T": w13T, "w2T": w2T, "wqkvT": wqkvT, "gwT": a["L0_ffn_gate_w"].T,
        "gate_b": np.tile(a["L0_ffn_gate_b"].reshape(1, NEXP), (P, 1)),
        "ident": np.eye(P, dtype=np.float32), "mask": mask, "cos": cos, "sin": sin,
    }
    arrays = {f"in_{k}": np.ascontiguousarray(v) for k, v in arrays.items()}
    nc = bacc.Bacc("TRN2", target_bir_lowering=False, num_devices=1)
    args = [nc.dram_tensor(k, v.shape, mybir.dt.from_np(v.dtype), kind="ExternalInput").ap() for k, v in arrays.items()]
    args.append(nc.dram_tensor("comb_rows", (2, NEXP, TILE), F32, kind="Internal").ap())
    args.append(nc.dram_tensor("out_x", (B, M, D), F32, kind="ExternalOutput").ap())
    macaron(nc, *args)
    r = run_bass_kernel_spmd(nc, [arrays], core_ids=[0])
    return r.results[0]["out_x"]
```
